# Optimizing a Trainium2 kernel written in Bass

```python
import numpy as np
import jax
import jax.numpy as jnp

def _softmax(x, axis=-1):
    return jax.nn.softmax(x, axis=axis)

def _gelu(x):
    return jax.nn.gelu(x, approximate=True)

def _silu(x):
    return jax.nn.silu(x)

def _sigmoid(x):
    return jax.nn.sigmoid(x)

def _layernorm(x, axis=-1, eps=1e-05):
    m = jnp.mean(x, axis=axis, keepdims=True)
    v = jnp.var(x, axis=axis, keepdims=True)
    return (x - m) / jnp.sqrt(v + eps)

def _scatter_add(tgt, idx, src, axis=0):
    return tgt.at[idx].add(src)

def _segment_sum(src, seg, n):
    return jax.ops.segment_sum(src, seg, n)
kernel_name = 'mk_flamingo_gated_d1_seqx_r4_c4e83a'

def setup_inputs(seed: int=0):
    np.random.seed(seed)
    _w = jnp.asarray

    def _rec_inputs():
        import jax
        import jax.numpy as jnp
        _rk = jax.random.key(seed)
        x = 7.22e-05 + 1 * jax.random.normal(jax.random.fold_in(_rk, 1), (8, 512, 256), jnp.float32)
        _lenS = 512 - jax.random.randint(jax.random.fold_in(_rk, 7), (8,), 0, max(1, 512 // 4) + 1, jnp.int32)
        _lenS2 = 512 - jax.random.randint(jax.random.fold_in(_rk, 8), (8,), 0, max(1, 512 // 4) + 1, jnp.int32)
        _ctx_1024P = jax.random.normal(jax.random.fold_in(_rk, 11), (8, 16, 256), jnp.float32)
        _ctx_1024c = jax.random.dirichlet(jax.random.fold_in(_rk, 511), 0.3 * jnp.ones((16,), jnp.float32), (8, 512))
        _ctx_1024t = jnp.einsum('bsk,bkd->bsd', _ctx_1024c, _ctx_1024P)
        _ctx_1024t = _ctx_1024t * jax.lax.rsqrt(jnp.mean(jnp.square(_ctx_1024t)) + 1e-12) * 0.953939
        ctx_1024 = 4.13588e-05 + 0.999923 * (_ctx_1024t + 0.3 * jax.random.normal(jax.random.fold_in(_rk, 611), (8, 512, 256), jnp.float32))
        _g = jax.random.normal(jax.random.fold_in(_rk, 9001), (2, 1), jnp.float32)
        _g = jnp.sign(_g) * jnp.maximum(jnp.abs(_g), 1.0) + (_g == 0) * 1.0
        g_xattn = _g[0]
        g_ffn = _g[1]
        return (x, ctx_1024, g_xattn, g_ffn)
    x, ctx_1024, g_xattn, g_ffn = _rec_inputs()

    def _L0_xattn_setup():
        import jax, jax.numpy as jnp
        import numpy as np
        D_EMB = 256
        N_HEADS = 16
        D_K = D_EMB // N_HEADS
        B, L = (4, 512)
        key = jax.random.key(seed)
        kx, kc, kq, kk, kv, ko = jax.random.split(key, 6)
        bound = float(np.sqrt(3.0 / D_EMB))
        uni = lambda k: jax.random.uniform(k, (D_EMB, D_EMB), jnp.float32, -bound, bound)
        return {'x': jax.random.normal(kx, (B, L, D_EMB), jnp.float32), 'context': jax.random.normal(kc, (B, L, D_EMB), jnp.float32), 'Wq': uni(kq), 'Wk': uni(kk), 'Wv': uni(kv), 'Wo': uni(ko)}
    _L0_xattn_all = _L0_xattn_setup()
    _L0_xattn_in = {k: v for k, v in _L0_xattn_all.items() if k in ('Wq', 'Wk', 'Wv', 'Wo')}
    del _L0_xattn_all

    def _L0_ffn_setup():
        import jax, jax.numpy as jnp
        import numpy as np
        H = 256
        I = 256
        E = 8
        key = jax.random.key(seed)
        ks = jax.random.split(key, 8)
        s = 0.02
        x = jax.random.normal(ks[0], (4, 512, H), dtype=jnp.float32)
        Wg = jax.random.normal(ks[1], (H, E), dtype=jnp.float32) * s
        bg = jnp.zeros((E,), dtype=jnp.float32)
        W1 = jax.random.normal(ks[2], (E, H, I), dtype=jnp.float32) * s
        b1 = jnp.zeros((E, I), dtype=jnp.float32)
        W2 = jax.random.normal(ks[3], (E, I, H), dtype=jnp.float32) * s
        b2 = jnp.zeros((E, H), dtype=jnp.float32)
        return {'x': x, 'Wg': Wg, 'bg': bg, 'W1': W1, 'b1': b1, 'W2': W2, 'b2': b2}
    _L0_ffn_all = _L0_ffn_setup()
    _L0_ffn_in = {k: v for k, v in _L0_ffn_all.items() if k in ('Wg', 'bg', 'W1', 'b1', 'W2', 'b2')}
    del _L0_ffn_all
    return {'x': x, 'ctx_1024': ctx_1024, 'g_xattn': g_xattn, 'g_ffn': g_ffn, 'L0_xattn_Wq': _L0_xattn_in['Wq'], 'L0_xattn_Wk': _L0_xattn_in['Wk'], 'L0_xattn_Wv': _L0_xattn_in['Wv'], 'L0_xattn_Wo': _L0_xattn_in['Wo'], 'L0_ffn_Wg': _L0_ffn_in['Wg'], 'L0_ffn_bg': _L0_ffn_in['bg'], 'L0_ffn_W1': _L0_ffn_in['W1'], 'L0_ffn_b1': _L0_ffn_in['b1'], 'L0_ffn_W2': _L0_ffn_in['W2'], 'L0_ffn_b2': _L0_ffn_in['b2']}

def reference(x, ctx_1024, g_xattn, g_ffn, L0_xattn_Wq, L0_xattn_Wk, L0_xattn_Wv, L0_xattn_Wo, L0_ffn_Wg, L0_ffn_bg, L0_ffn_W1, L0_ffn_b1, L0_ffn_W2, L0_ffn_b2):
    import jax
    import jax.numpy as jnp

    def _L0_xattn_ref(x, context, Wq, Wk, Wv, Wo):
        import jax, jax.numpy as jnp
        import numpy as np
        D_EMB = 256
        N_HEADS = 16
        D_K = D_EMB // N_HEADS
        B, L = (4, 512)
        b, length, d = x.shape
        Q = (x @ Wq.T).reshape(b, length, N_HEADS, D_K).swapaxes(-2, -1)
        K = (context @ Wk.T).reshape(b, length, N_HEADS, D_K).swapaxes(-2, -1)
        V = (context @ Wv.T).reshape(b, length, N_HEADS, D_K).swapaxes(-2, -1)
        qk = jnp.einsum('blih,bljh->blij', Q, K) / jnp.sqrt(jnp.asarray(D_K, x.dtype))
        attn = jax.nn.softmax(qk, axis=-1)
        valued = jnp.einsum('blij,bljh->blih', attn, V)
        concat = valued.swapaxes(-2, -1).reshape(b, length, d)
        return concat @ Wo.T

    def _L0_ffn_ref(x, Wg, bg, W1, b1, W2, b2):
        import jax, jax.numpy as jnp
        import numpy as np
        H = 256
        I = 256
        E = 8
        B, S, Hd = x.shape
        xf = x.reshape(-1, Hd)
        logits = xf @ Wg + bg
        gates = jax.nn.softmax(logits, axis=-1)
        idx = jnp.argmax(gates, axis=-1)
        h = jax.nn.gelu(jnp.einsum('th,ehi->tei', xf, W1) + b1, approximate=False)
        y = jnp.einsum('tei,eih->teh', h, W2) + b2
        out = jnp.take_along_axis(y, idx[:, None, None], axis=1)[:, 0, :]
        return out.reshape(B, S, Hd)
    x = x + jnp.tanh(g_xattn[0]) * _L0_xattn_ref(_layernorm(x, axis=-1), ctx_1024, L0_xattn_Wq, L0_xattn_Wk, L0_xattn_Wv, L0_xattn_Wo)
    x = x + jnp.tanh(g_ffn[0]) * _L0_ffn_ref(_layernorm(x, axis=-1), L0_ffn_Wg, L0_ffn_bg, L0_ffn_W1, L0_ffn_b1, L0_ffn_W2, L0_ffn_b2)
    return x

_drawn_inputs = setup_inputs


def setup_inputs(seed=0):
    import zlib

    import numpy as np

    out = dict(_drawn_inputs(seed))
    spreads = {'L0_ffn_bg': (0.0, 0.1), 'L0_ffn_b1': (0.0, 0.493), 'L0_ffn_b2': (0.0, 0.1)}
    factors = {}
    for name, (base, spread) in spreads.items():
        noise = np.random.default_rng([zlib.crc32(name.encode()), seed]).standard_normal(out[name].shape)
        drawn = base * np.exp(spread * noise) if base else spread * noise
        out[name] = jnp.asarray(drawn.astype(out[name].dtype))
    for name, factor in factors.items():
        out[name] = (out[name] * factor).astype(out[name].dtype)
    return out
```

```python
from contextlib import ExitStack

import concourse.bass as bass
from concourse import mybir

ALU = mybir.AluOpType
ACT = mybir.ActivationFunctionType
AX = mybir.AxisListType
F32 = mybir.dt.float32
BF16 = mybir.dt.bfloat16
I32 = mybir.dt.int32
U32 = mybir.dt.uint32

P = 128
D = 256
KC = D // P
H = 16
EPS = 1e-5
GB = 4
T8 = 8
E = 8
ROW = D + 4
C_ID, C_TRI, C_MASK, C_REV, C_BASE, C_TRI8 = 0, P, 2 * P, 2 * P + 8, 2 * P + 16, 2 * P + 24
C_LANE = C_TRI8 + 64
C_TOK = C_LANE + 1
C_NUM = C_TOK + 32
C_BLK = C_NUM + 32


def wait(eng, sem, value):
    if isinstance(value, int) and value <= 0:
        return
    eng.wait_ge(sem, value)


def wait_apart(eng, sem, value, passed):
    if isinstance(value, int) and value <= 0:
        return
    eng.wait_ge(sem, value)
    eng.sem_inc(passed, 1)


class Steps:

    def __init__(self, eng, sem, call, per_call):
        self.eng, self.sem, self.base, self.per, self.at = eng, sem, call * per_call, per_call, 0

    def then(self, ins, passed=None):
        ins.then_inc(self.sem, 1)
        self.at += 1
        assert self.at <= self.per
        if passed is None:
            self.eng.wait_ge(self.sem, self.base + self.at)
        else:
            wait_apart(self.eng, self.sem, self.base + self.at, passed)


def flamingo_block(nc, x, ctx_t, g_x, g_f, w_qkvo, wg, bg, w1b, w2, b2, consts, out):
    tokens = x.shape[0]
    tiles = tokens // P
    pairs = tiles // 2
    region = tokens + P
    blocks = tiles + E
    x_v = x.rearrange("(p j) d -> p j d", p=P)
    rows = nc.dram_tensor("routed_rows", (E * region + P, ROW), F32).ap()

    with ExitStack() as stack:
        def sb(name, shape, dt=F32):
            return stack.enter_context(nc.sbuf_tensor("sb_" + name, shape, dt))

        def ps(name, shape):
            return stack.enter_context(nc.psum_tensor("ps_" + name, shape, F32))

        def sem(name):
            return stack.enter_context(nc.semaphore(name))

        cst = sb("cst", [P, C_BLK + blocks])
        wt = sb("wt", [P, 4, KC, D])
        wg_sb = sb("wg", [P, KC, E])
        bg_sb = sb("bg", [P, E])
        w2_sb = sb("w2", [P, E, KC, D])
        b2_sb = sb("b2", [P, E, D])
        gates = sb("gates", [P, 2])
        tg = sb("tg", [P, 2])
        tri = sb("tri", [P, P], BF16)
        ones = sb("ones", [P, P], BF16)
        neg_half = sb("neg_half", [P, 2])
        x_sb = sb("x", [P, tiles, D])
        ct = sb("ct", [P, KC, 2, P])
        st = sb("st", [P, 2, 6])
        mv = sb("mv", [P, 2, 2])
        ve = sb("ve", [P, 2])
        rstd = sb("rstd", [P, 2])
        xn = sb("xn", [P, 2, D])
        xt = sb("xt", [P, KC, 2, P])
        y_q = sb("y_q", [P, 32, H])
        y_k = sb("y_k", [P, 32, H])
        y_v = sb("y_v", [P, 32, H])
        qt = sb("qt", [P, 32, H])
        kt = sb("kt", [P, 32, H])
        vt = sb("vt", [P, 32, H])
        kb = sb("kb", [P, 32, T8, H])
        vb = sb("vb", [P, 32, T8, H])
        mx = sb("mx", [P, 2, 32])
        pe_x = sb("pe_x", [P, 2, 512])
        sm = sb("sm", [P, 2, 32])
        rs = sb("rs", [P, 2, 32])
        rt = sb("rt", [P, 2, 32])
        at = sb("at", [P, 2, GB, 4, H])
        om = sb("om", [P, 2, H, 32])
        cn = sb("cn", [P, 2, H, H])
        ot = sb("ot", [P, KC, 2, P])
        xs = sb("xs", [P, 2, ROW])
        st1 = sb("st1", [P, 2, 6])
        ve1 = sb("ve1", [P, 2])
        x1n = sb("x1n", [P, 2, D])
        x1t = sb("x1t", [P, KC, 2, P])
        lg = sb("lg", [P, 2, E])
        lm = sb("lm", [P, 2])
        le = sb("le", [P, 2, E])
        lw = sb("lw", [P, 2])
        oh = sb("oh", [P, 2, E])
        oh_b = sb("oh_b", [P, 2, E], BF16)
        base = sb("base", [P, E])
        rb = sb("rb", [P, 2, E])
        tot = sb("tot", [P, 2, E])
        pos = sb("pos", [P, 2])
        pos_i = sb("pos_i", [P, 2], U32)
        pad_row = sb("pad_row", [P, ROW])
        pad_i = sb("pad_i", [P, E], U32)
        cnt = sb("cnt", [P, E])
        nbm = sb("nbm", [P, E, 32])
        nb = sb("nb", [P, E])
        cmm = sb("cmm", [P, E, E])
        cum = sb("cum", [P, 2, E])
        org = sb("org", [P, E])
        bm = sb("bm", [P, 3, blocks, E])
        br = sb("br", [P, 4, blocks])
        tab = sb("tab", [P, 2, blocks], I32)
        w1_sb = [sb(f"w1_{i}", [P, KC * D + KC]) for i in range(2)]
        xb = [sb(f"xb_{i}", [P, ROW]) for i in range(4)]
        xbn = [sb(f"xbn_{i}", [P, D]) for i in range(2)]
        xbt = [sb(f"xbt_{i}", [P, KC, P]) for i in range(2)]
        ht = [sb(f"ht_{i}", [P, KC, P]) for i in range(2)]
        yo = [sb(f"yo_{i}", [P, D]) for i in range(2)]
        yf = [sb(f"yf_{i}", [P, D]) for i in range(2)]
        tok_i = [sb(f"tok_i_{i}", [P, 1], U32) for i in range(2)]

        tr = [ps(f"tr{i}", [P, 512]) for i in range(2)]
        pr = [ps(f"pr{i}", [P, 512]) for i in range(2)]
        s_ps = ps("s", [P, 1024])
        o_ps = ps("o", [P, 1024])

        cst_in, wt_in, gate_in, late_in = sem("cst_in"), sem("wt_in"), sem("gate_in"), sem("late_in")
        x_in, ct_in = sem("x_in"), sem("ct_in")
        setup_step, consts_ok, zero_ok = sem("setup_step"), sem("consts_ok"), sem("zero_ok")
        tanh_ok = sem("tanh_ok")
        passed_dve, passed_pool = sem("passed_dve"), sem("passed_pool")
        ln_step, ln_var, ln_pow, ln_done = sem("ln_step"), sem("ln_var"), sem("ln_pow"), sem("ln_done")
        xt_done, xt_out = sem("xt_done"), sem("xt_out")
        q_done, k_done, v_done = sem("q_done"), sem("k_done"), sem("v_done")
        yq_out, yk_out, yv_out = sem("yq_out"), sem("yk_out"), sem("yv_out")
        qt_done, kt_done, vt_done = sem("qt_done"), sem("kt_done"), sem("vt_done")
        qt_out, kt_out, vt_out = sem("qt_out"), sem("kt_out"), sem("vt_out")
        kb_done, vb_done = sem("kb_done"), sem("vb_done")
        score_done = sem("score_done")
        max_done, sub_done, exp_done = sem("max_done"), sem("sub_done"), sem("exp_done")
        at_done, at_out = sem("at_done"), sem("at_out")
        sum_step, rt_done = sem("sum_step"), sem("rt_done")
        av_done = sem("av_done")
        om_done = sem("om_done")
        cn_done, ot_done, ot_out, wo_done = sem("cn_done"), sem("ot_done"), sem("ot_out"), sem("wo_done")
        res_step, res_var, res_pow, res_done = sem("res_step"), sem("res_var"), sem("res_pow"), sem("res_done")
        x1t_done, x1t_out, lg_done = sem("x1t_done"), sem("x1t_out"), sem("lg_done")
        pick_step, oh_done, rank_done = sem("pick_step"), sem("oh_done"), sem("rank_done")
        pos_step, rank_read, pos_done = sem("pos_step"), sem("rank_read"), sem("pos_done")
        routed = sem("routed")
        pad_done, pad_in = sem("pad_done"), sem("pad_in")
        tab_step, tab_done = sem("tab_step"), sem("tab_done")
        xb_in = [sem(f"xb_in{i}") for i in range(4)]
        w1_in = [sem(f"w1_in{i}") for i in range(2)]
        xbn_done, xbt_done, xbt_out = sem("xbn_done"), sem("xbt_done"), sem("xbt_out")
        h_done, gelu_done = sem("h_done"), sem("gelu_done")
        y_done, yb_done, yf_done = sem("y_done"), sem("yb_done"), sem("yf_done")
        stored = [sem(f"stored{i}") for i in range(2)]

        ident = cst[:, C_ID:C_ID + P]
        block = stack.enter_context(nc.Block())

        def slots(eng, pre, slot):
            pre()
            slot(0)
            slot(1)
            with eng.Fori(2, pairs - 1) as k:
                slot(k)
            slot(pairs - 1)
            slot(pairs)
            slot(pairs + 1)

        def has(k, shift):
            return not isinstance(k, int) or 0 <= k + shift < pairs

        def block_slots(eng, slot, skew):
            for b in range(4):
                slot(b, b, 0)
            with eng.Fori(1, blocks // 4 - 1) as turn:
                for q in range(4):
                    slot(4 * turn + q, q, turn)
            for b in range(blocks - 4, blocks + skew):
                slot(b, b % 4, b // 4)

        @block.sync
        def _(sp):
            def pre():
                sp.dma_start(cst[:], consts).then_inc(cst_in, 16)
                sp.dma_start(x_sb[:, 0:2, :], x_v[:, 0:2, :]).then_inc(x_in, 16)
                sp.dma_start(ct[:].rearrange("p a b c -> p (a b c)"), ctx_t[0]).then_inc(ct_in, 16)
                sp.dma_start(wt[:], w_qkvo).then_inc(wt_in, 16)
                sp.dma_start(gates[:, 0:1], g_x.partition_broadcast(P)).then_inc(gate_in, 16)
                sp.dma_start(gates[:, 1:2], g_f.partition_broadcast(P)).then_inc(gate_in, 16)
                sp.dma_start(wg_sb[:], wg).then_inc(gate_in, 16)
                sp.dma_start(bg_sb[:], bg.partition_broadcast(P)).then_inc(gate_in, 16)

            def load(n):
                sp.wait_ge(x_in, 16 * n)
                sp.dma_start(x_sb[:, bass.ds(2 * n, 2), :], x_v[:, bass.ds(2 * n, 2), :]).then_inc(x_in, 16)
                sp.wait_ge(v_done, n)
                sp.dma_start(ct[:].rearrange("p a b c -> p (a b c)"),
                             ctx_t[bass.ds(n, 1)].rearrange("a p f -> p (a f)")).then_inc(ct_in, 16)

            pre()
            load(1)
            sp.dma_start(w2_sb[:], w2).then_inc(late_in, 16)
            sp.dma_start(b2_sb[:].rearrange("p e d -> p (e d)"), b2.partition_broadcast(P)).then_inc(late_in, 16)
            with sp.Fori(2, pairs) as n:
                load(n)

            sp.wait_ge(tab_done, 1)
            sp.wait_ge(routed, 32 * pairs)
            sp.wait_ge(pad_in, 16 * (E + 1))

            def fetch(b, q, turn):
                i = q % 2
                row = sp.value_load(tab[0:1, 0, bass.ds(b, 1)], min_val=0, max_val=E * region)
                ex = sp.value_load(tab[0:1, 1, bass.ds(b, 1)], min_val=0, max_val=E - 1)
                wait(sp, yf_done, b - 3)
                sp.dma_start(xb[q][:], rows[bass.ds(row, P), :]).then_inc(xb_in[q], 16)
                wait(sp, h_done, b - 1)
                wait(sp, gelu_done, b - 1)
                sp.dma_start(w1_sb[i][:], w1b[bass.ds(ex, 1)].rearrange("a p f -> p (a f)")).then_inc(w1_in[i], 16)

            block_slots(sp, fetch, 0)
            for i in range(2):
                sp.wait_ge(stored[i], 8 * blocks)

        @block.tensor
        def _(pe):
            def transpose_x(n):
                pe.wait_ge(ln_done, n + 1)
                wait(pe, vt_out, n)
                for kc in range(KC):
                    for s in range(2):
                        q = (kc * 2 + s) * P
                        last = pe.transpose(tr[0][:, q:q + P], xn[:, s, kc * P:(kc + 1) * P], ident)
                last.then_inc(xt_done, 1)

            def project(src, w, bank, done):
                for s in range(2):
                    for kc in range(KC):
                        last = pe.matmul(pr[bank][:, s * D:(s + 1) * D], lhsT=src[:, kc, s, :],
                                         rhs=wt[:, w, kc, :], start=(kc == 0), stop=(kc == KC - 1))
                last.then_inc(done, 1)

            def project_q(n):
                pe.wait_ge(xt_out, n + 1)
                wait(pe, yv_out, n)
                wait(pe, oh_done, n - 2)
                project(xt, 0, 0, q_done)

            def project_k(n):
                pe.wait_ge(ct_in, 16 * (n + 1))
                wait(pe, yk_out, n)
                wait(pe, rank_read, n - 2)
                project(ct, 1, 1, k_done)

            def project_v(n):
                pe.wait_ge(yq_out, n + 1)
                project(ct, 2, 0, v_done)

            def transpose_y(y, bank, done):
                for g in range(GB):
                    last = pe.transpose(tr[bank][:, g * P:(g + 1) * P],
                                        y[:, T8 * g:T8 * (g + 1), :].rearrange("p t h -> p (t h)"), ident)
                last.then_inc(done, 1)

            def transpose_q(n):
                pe.wait_ge(yq_out, n + 1)
                transpose_y(y_q, 0, qt_done)

            def transpose_k(n):
                pe.wait_ge(yk_out, n + 1)
                wait(pe, at_out, 2 * n - 1)
                transpose_y(y_k, 1, kt_done)

            def transpose_v(n):
                pe.wait_ge(yv_out, n + 1)
                wait(pe, at_out, 2 * n)
                pe.wait_ge(qt_out, n + 1)
                transpose_y(y_v, 0, vt_done)

            def scores(n):
                pe.wait_ge(qt_out, n + 1)
                pe.wait_ge(kb_done, n + 1)
                wait(pe, sub_done, 2 * n)
                if isinstance(n, int) and n == 0:
                    pe.wait_ge(zero_ok, 1)
                for s in range(2):
                    for g in range(GB):
                        for c in range(4):
                            i = (g * 4 + c) * 2 + s
                            q = s * 512 + g * P
                            last = pe.matmul(s_ps[32 * c:32 * c + H, q:q + P], lhsT=qt[:, i, :],
                                             rhs=kb[:, i, :, :].rearrange("p t j -> p (t j)"),
                                             start=True, stop=True)
                    last.then_inc(score_done, 1)

            def transpose_a(n, more):
                for s, bank in ((0, 1), (1, 0)):
                    pe.wait_ge(exp_done, 2 * n + s + 1)
                    if s == 0:
                        pe.wait_ge(kt_out, n + 1)
                    else:
                        pe.wait_ge(vt_out, n + 1)
                        if more:
                            pe.wait_ge(qt_out, n + 2)
                    for g in range(GB):
                        last = pe.transpose(tr[bank][:, g * P:(g + 1) * P],
                                            pe_x[:, s, g * P:(g + 1) * P], ident)
                    last.then_inc(at_done, 1)

            def values(n):
                pe.wait_ge(vb_done, n + 1)
                wait(pe, om_done, 2 * n)
                for s in range(2):
                    pe.wait_ge(at_out, 2 * n + s + 1)
                    for g in range(GB):
                        for c in range(4):
                            i = (g * 4 + c) * 2 + s
                            q = s * 512 + g * P
                            last = pe.matmul(o_ps[32 * c:32 * c + H, q:q + P], lhsT=at[:, s, g, c, :],
                                             rhs=vb[:, i, :, :].rearrange("p t h -> p (t h)"),
                                             start=True, stop=True)
                    last.then_inc(av_done, 1)

            def transpose_o(n):
                pe.wait_ge(cn_done, n + 1)
                wait(pe, x1t_out, n)
                for kc in range(KC):
                    for s in range(2):
                        q = (kc * 2 + s) * P
                        last = pe.transpose(tr[1][:, q:q + P],
                                            cn[:, s, 8 * kc:8 * kc + 8, :].rearrange("p h i -> p (h i)"), ident)
                last.then_inc(ot_done, 1)

            def project_o(n, more):
                pe.wait_ge(ot_out, n + 1)
                if more:
                    pe.wait_ge(yk_out, n + 3)
                wait(pe, rank_read, n)
                project(ot, 3, 1, wo_done)

            def transpose_x1(n, more):
                pe.wait_ge(res_done, n + 1)
                if more:
                    pe.wait_ge(kt_out, n + 3)
                wait(pe, at_out, min(2 * n + 3, 2 * pairs) if isinstance(n, int) else 2 * n + 3)
                for kc in range(KC):
                    for s in range(2):
                        q = (kc * 2 + s) * P
                        last = pe.transpose(tr[1][:, q:q + P], x1n[:, s, kc * P:(kc + 1) * P], ident)
                last.then_inc(x1t_done, 1)

            def logits(n, more):
                pe.wait_ge(x1t_out, n + 1)
                if more:
                    pe.wait_ge(yv_out, n + 3)
                wait(pe, oh_done, n)
                for s in range(2):
                    for kc in range(KC):
                        last = pe.matmul(pr[0][:, s * E:(s + 1) * E], lhsT=x1t[:, kc, s, :],
                                         rhs=wg_sb[:, kc, :], start=(kc == 0), stop=(kc == KC - 1))
                last.then_inc(lg_done, 1)

            def ranks(n):
                pe.wait_ge(oh_done, n + 1)
                rhs = oh_b[:].rearrange("p s e -> p (s e)")
                pe.matmul(pr[1][:, 0:2 * E], lhsT=tri[:], rhs=rhs, start=True, stop=True)
                pe.matmul(pr[1][:, 2 * E:4 * E], lhsT=ones[:], rhs=rhs, start=True, stop=True).then_inc(rank_done, 1)

            def slot(k):
                more = has(k, 1)
                if has(k, 0):
                    scores(k)
                if has(k, -2):
                    ranks(k - 2)
                if more:
                    transpose_x(k + 1)
                if has(k, -1):
                    transpose_o(k - 1)
                if more:
                    project_q(k + 1)
                    project_k(k + 1)
                    project_v(k + 1)
                if has(k, -1):
                    project_o(k - 1, more)
                if more:
                    transpose_q(k + 1)
                if has(k, 0):
                    transpose_a(k, more)
                if more:
                    transpose_k(k + 1)
                    transpose_v(k + 1)
                if has(k, 0):
                    values(k)
                if has(k, -1):
                    transpose_x1(k - 1, more)
                    logits(k - 1, more)

            def pre():
                pe.wait_ge(cst_in, 16)
                transpose_x(0)
                pe.wait_ge(wt_in, 16)
                project_q(0)
                project_k(0)
                project_v(0)
                transpose_q(0)
                transpose_k(0)
                transpose_v(0)
                pe.wait_ge(gate_in, 64)
                pe.wait_ge(consts_ok, 1)

            slots(pe, pre, slot)

            def transpose_b(b, i):
                pe.wait_ge(xbn_done, b + 1)
                wait(pe, xbt_out, b - 1)
                for kc in range(KC):
                    last = pe.transpose(tr[i][:, kc * P:(kc + 1) * P], xbn[i][:, kc * P:(kc + 1) * P], ident)
                last.then_inc(xbt_done, 1)

            def layer1(b, i, nth):
                pe.wait_ge(xbt_out, b + 1)
                pe.wait_ge(w1_in[i], 16 * (nth + 1))
                wait(pe, gelu_done, b - 1)
                for ic in range(KC):
                    for kc in range(KC):
                        last = pe.matmul(pr[i][:, ic * P:(ic + 1) * P],
                                         lhsT=w1_sb[i][:, kc * D + ic * P:kc * D + (ic + 1) * P],
                                         rhs=xbt[i][:, kc, :], start=(kc == 0), stop=(kc == KC - 1))
                last.then_inc(h_done, 1)

            def layer2(b, i):
                ex = pe.value_load(tab[0:1, 1, bass.ds(b, 1)], min_val=0, max_val=E - 1)
                pe.wait_ge(gelu_done, b + 1)
                wait(pe, yb_done, b - 1)
                for ic in range(KC):
                    last = pe.matmul(o_ps[:, 512 * i:512 * i + D], lhsT=ht[i][:, ic, :],
                                     rhs=w2_sb[:, bass.ds(ex, 1), ic, :].rearrange("p a d -> p (a d)"),
                                     start=(ic == 0), stop=(ic == KC - 1))
                last.then_inc(y_done, 1)

            pe.wait_ge(late_in, 32)
            pe.wait_ge(tab_done, 1)
            transpose_b(0, 0)

            def expert_slot(b, q, turn):
                i = q % 2
                known = isinstance(b, int)
                if not known or b < blocks:
                    layer1(b, i, 2 * turn + q // 2)
                if not known or b + 1 < blocks:
                    transpose_b(b + 1, 1 - i)
                if not known or b > 0:
                    layer2(b - 1, 1 - i)

            block_slots(pe, expert_slot, 1)

        @block.scalar
        def _(act):
            def copy_xt(n):
                act.wait_ge(xt_done, n + 1)
                wait(act, q_done, n)
                act.copy(xt[:].rearrange("p a b c -> p (a b c)"), tr[0][:]).then_inc(xt_out, 1)

            def copy_qt(n):
                act.wait_ge(qt_done, n + 1)
                wait(act, score_done, 2 * n)
                act.copy(qt[:].rearrange("p a b -> p (a b)"), tr[0][:]).then_inc(qt_out, 1)

            def copy_kt(n):
                act.wait_ge(kt_done, n + 1)
                wait(act, kb_done, n)
                act.copy(kt[:].rearrange("p a b -> p (a b)"), tr[1][:]).then_inc(kt_out, 1)

            def copy_vt(n):
                act.wait_ge(vt_done, n + 1)
                wait(act, vb_done, n)
                act.copy(vt[:].rearrange("p a b -> p (a b)"), tr[0][:]).then_inc(vt_out, 1)

            def exps(n, s):
                act.wait_ge(sub_done, 2 * n + s + 1)
                act.activation(pe_x[:, s, :], pe_x[:, s, :], ACT.Exp, scale=float(H) ** -0.5).then_inc(exp_done, 1)

            def copy_at(n, s):
                act.wait_ge(at_done, 2 * n + s + 1)
                wait(act, av_done, 2 * n)
                act.copy(at[:, s].rearrange("p g c i -> p (g c) i"),
                         tr[1 - s][:].rearrange("p (q w) -> p q w", w=32)[:, :, 0:H]).then_inc(at_out, 1)

            def copy_ot(n):
                act.wait_ge(ot_done, n + 1)
                wait(act, wo_done, n)
                act.copy(ot[:].rearrange("p a b c -> p (a b c)"), tr[1][:]).then_inc(ot_out, 1)

            def copy_x1t(n):
                act.wait_ge(x1t_done, n + 1)
                wait(act, lg_done, n)
                act.copy(x1t[:].rearrange("p a b c -> p (a b c)"), tr[1][:]).then_inc(x1t_out, 1)

            def slot(k):
                more = has(k, 1)
                if has(k, 0):
                    exps(k, 0)
                if more:
                    copy_xt(k + 1)
                if has(k, -1):
                    copy_ot(k - 1)
                if has(k, 0):
                    exps(k, 1)
                if more:
                    copy_qt(k + 1)
                if has(k, 0):
                    copy_at(k, 0)
                    copy_at(k, 1)
                if more:
                    copy_kt(k + 1)
                    copy_vt(k + 1)
                if has(k, -1):
                    copy_x1t(k - 1)

            def pre():
                act.wait_ge(gate_in, 64)
                act.activation(tg[:], gates[:], ACT.Tanh).then_inc(tanh_ok, 1)
                copy_xt(0)
                copy_qt(0)
                copy_kt(0)
                copy_vt(0)

            slots(act, pre, slot)

            def expert_slot(b, q, turn):
                i = q % 2
                known = isinstance(b, int)
                if not known or b < blocks:
                    act.wait_ge(h_done, b + 1)
                    wait(act, y_done, b - 1)
                    for ic in range(KC):
                        last = act.activation(ht[i][:, ic, :], pr[i][:, ic * P:(ic + 1) * P], ACT.Gelu,
                                              bias=w1_sb[i][:, KC * D + ic:KC * D + ic + 1])
                    last.then_inc(gelu_done, 1)
                if not known or b + 1 < blocks:
                    copy_xbt(b + 1, 1 - i)

            def copy_xbt(b, i):
                act.wait_ge(xbt_done, b + 1)
                wait(act, h_done, b - 1)
                act.copy(xbt[i][:].rearrange("p a b -> p (a b)"), tr[i][:, 0:KC * P]).then_inc(xbt_out, 1)

            copy_xbt(0, 0)
            block_slots(act, expert_slot, 0)

        @block.vector
        def _(dve):
            def norm_x(n):
                step = Steps(dve, ln_step, n, 3)
                dve.wait_ge(x_in, 16 * (n + 1))
                for s in range(2):
                    last = dve.bn_stats(st[:, s, :], x_sb[:, bass.ds(2 * n + s, 1), :].rearrange("p a d -> p (a d)"))
                step.then(last, passed_dve)
                for s in range(2):
                    last = dve.bn_aggr(mv[:, s, :], st[:, s, :])
                step.then(last)
                dve.tensor_scalar(ve[:], mv[:, :, 1], EPS, None, ALU.add).then_inc(ln_var, 1)
                dve.wait_ge(ln_pow, n + 1)
                wait(dve, xt_done, n)
                for s in range(2):
                    last = dve.tensor_scalar(xn[:, s, :], x_sb[:, bass.ds(2 * n + s, 1), :].rearrange("p a d -> p (a d)"),
                                             mv[:, s, 0:1], rstd[:, s:s + 1], ALU.subtract, ALU.mult)
                last.then_inc(ln_done, 1)
                step.then(dve.memset(st[:, 0, 0:1], 0.0))

            def turn_qk(n, done, done_t, y, bank, out_sem):
                dve.wait_ge(done, n + 1)
                wait(dve, done_t, n)
                dve.transpose(y[:].rearrange("p t h -> p h t"),
                              pr[bank][:].rearrange("p (s h i) -> p h s i", s=2, h=H)).then_inc(out_sem, 1)

            def turn_v(n):
                dve.wait_ge(v_done, n + 1)
                wait(dve, vt_done, n)
                dve.transpose(y_v[:].rearrange("p t j -> p j t"),
                              pr[0][:].rearrange("p (s h j) -> p j s h", s=2, h=H)).then_inc(yv_out, 1)

            def spread_k(n):
                dve.wait_ge(kt_out, n + 1)
                wait(dve, score_done, 2 * n)
                for t in range(T8):
                    last = dve.tensor_scalar(kb[:, :, t, :], kt[:], cst[:, C_MASK + t:C_MASK + t + 1], None, ALU.mult)
                last.then_inc(kb_done, 1)

            def shift(n, s):
                dve.wait_ge(score_done, 2 * n + s + 1)
                sv = s_ps[:, 512 * s:512 * (s + 1)].rearrange("p (t j) -> p t j", j=H)
                dve.tensor_reduce(mx[:, s, :], sv, AX.X, ALU.max).then_inc(max_done, 1)
                wait(dve, at_done, 2 * n)
                dve.wait_ge(max_done, 2 * n + s + 1)
                dve.tensor_tensor(pe_x[:, s, :].rearrange("p (t j) -> p t j", j=H), sv,
                                  mx[:, s, :].unsqueeze(2).broadcast_to([P, 32, H]), ALU.subtract).then_inc(sub_done, 1)

            def sums(n):
                step = Steps(dve, sum_step, n, 2)
                dve.wait_ge(exp_done, 2 * n + 2)
                step.then(dve.tensor_reduce(sm[:], pe_x[:].rearrange("p s (t j) -> p s t j", j=H), AX.X, ALU.add))
                step.then(dve.reciprocal(rs[:], sm[:]))
                wait(dve, cn_done, n)
                dve.transpose(rt[:].rearrange("p s t -> p (s t)"), rs[:].rearrange("p s t -> p (s t)")).then_inc(rt_done, 1)

            def turn_o(n):
                wait(dve, cn_done, n)
                for s in range(2):
                    dve.wait_ge(av_done, 2 * n + s + 1)
                    dve.transpose(om[:, s], o_ps[:, 512 * s:512 * (s + 1)].rearrange("p (t h) -> p h t", h=H)).then_inc(om_done, 1)

            def residual(n):
                step = Steps(dve, res_step, n, 3)
                dve.wait_ge(wo_done, n + 1)
                wait(dve, routed, 32 * n)
                step.then(dve.scalar_tensor_tensor(xs[:, :, 0:D], pr[1][:].rearrange("p (s d) -> p s d", s=2), tg[:, 0:1],
                                                   x_sb[:, bass.ds(2 * n, 2), :], ALU.mult, ALU.add))
                for s in range(2):
                    last = dve.bn_stats(st1[:, s, :], xs[:, s, 0:D])
                step.then(last, passed_dve)
                for s in range(2):
                    last = dve.bn_aggr(xs[:, s, D:D + 2], st1[:, s, :])
                step.then(last)
                dve.tensor_scalar(ve1[:], xs[:, :, D + 1], EPS, None, ALU.add).then_inc(res_var, 1)
                dve.tensor_copy(xs[:, :, D + 2], cst[:, bass.ds(C_TOK + 2 * n, 2)])
                dve.wait_ge(res_pow, n + 1)
                wait(dve, x1t_done, n)
                for s in range(2):
                    last = dve.tensor_scalar(x1n[:, s, :], xs[:, s, 0:D], xs[:, s, D:D + 1], xs[:, s, D + 1:D + 2],
                                             ALU.subtract, ALU.mult)
                last.then_inc(res_done, 1)

            def wide(ap):
                return ap.unsqueeze(1).broadcast_to([P, 2, E])

            def deep(ap):
                return ap.unsqueeze(2).broadcast_to([P, 2, E])

            def pick(n):
                step = Steps(dve, pick_step, n, 5)
                dve.wait_ge(lg_done, n + 1)
                step.then(dve.tensor_tensor(lg[:], pr[0][:, 0:2 * E].rearrange("p (s e) -> p s e", s=2), wide(bg_sb[:]), ALU.add))
                step.then(dve.tensor_reduce(lm[:], lg[:], AX.X, ALU.max))
                step.then(dve.tensor_tensor(lg[:], lg[:], deep(lm[:]), ALU.is_equal))
                step.then(dve.tensor_tensor(le[:], lg[:], wide(cst[:, C_REV:C_REV + E]), ALU.mult))
                step.then(dve.tensor_reduce(lw[:], le[:], AX.X, ALU.max))
                wait(dve, rank_done, n)
                dve.tensor_tensor(oh[:], le[:], deep(lw[:]), ALU.is_equal)
                dve.tensor_tensor(oh_b[:], le[:], deep(lw[:]), ALU.is_equal).then_inc(oh_done, 1)

            def place(n):
                step = Steps(dve, pos_step, n, 6)
                dve.wait_ge(rank_done, n + 1)
                dve.tensor_copy(tot[:].rearrange("p s e -> p (s e)"), pr[1][:, 2 * E:4 * E])
                step.then(dve.tensor_tensor(rb[:], pr[1][:, 0:2 * E].rearrange("p (s e) -> p s e", s=2), wide(base[:]), ALU.add))
                dve.sem_inc(rank_read, 1)
                step.then(dve.tensor_tensor(rb[:, 1, :], rb[:, 1, :], tot[:, 0, :], ALU.add))
                step.then(dve.tensor_tensor(rb[:], rb[:], oh[:], ALU.mult))
                step.then(dve.tensor_reduce(pos[:], rb[:], AX.X, ALU.add))
                dve.tensor_copy(pos_i[:], pos[:]).then_inc(pos_done, 1)
                step.then(dve.tensor_tensor(base[:], base[:], tot[:, 0, :], ALU.add))
                step.then(dve.tensor_tensor(base[:], base[:], tot[:, 1, :], ALU.add))

            def slot(k):
                more = has(k, 1)
                if has(k, -1):
                    turn_o(k - 1)
                if has(k, 0):
                    shift(k, 0)
                    shift(k, 1)
                if has(k, -2):
                    place(k - 2)
                if more:
                    turn_qk(k + 1, q_done, qt_done, y_q, 0, yq_out)
                    turn_qk(k + 1, k_done, kt_done, y_k, 1, yk_out)
                    turn_v(k + 1)
                if has(k, 0):
                    sums(k)
                if has(k, -1):
                    residual(k - 1)
                if more:
                    spread_k(k + 1)
                if has(k, 2):
                    norm_x(k + 2)
                if has(k, -1):
                    pick(k - 1)

            def pre():
                step = Steps(dve, setup_step, 0, 2)
                dve.memset(neg_half[:], -0.5)
                dve.memset(xs[:], 0.0)
                dve.memset(ones[:], 1.0)
                dve.memset(pad_row[:], 0.0)
                dve.memset(s_ps[:], 0.0)
                step.then(dve.memset(o_ps[:], 0.0))
                dve.memset(pad_row[:, D + 2:D + 3], 2.0 * tokens)
                dve.wait_ge(cst_in, 16)
                dve.tensor_copy(tri[:], cst[:, C_TRI:C_TRI + P])
                step.then(dve.tensor_copy(base[:], cst[:, C_BASE:C_BASE + E]))
                dve.sem_inc(zero_ok, 1)
                dve.sem_inc(consts_ok, 1)
                norm_x(0)
                turn_qk(0, q_done, qt_done, y_q, 0, yq_out)
                turn_qk(0, k_done, kt_done, y_k, 1, yk_out)
                turn_v(0)
                spread_k(0)
                norm_x(1)
                dve.wait_ge(gate_in, 64)
                dve.wait_ge(tanh_ok, 1)

            def slot_(k):
                slot(k)

            pre()
            slot_(0)
            slot_(1)
            with dve.Fori(2, pairs - 2) as k:
                slot_(k)
            for k in range(pairs - 2, pairs + 2):
                slot_(k)

            step = Steps(dve, tab_step, 0, 17)
            step.then(dve.tensor_tensor(cnt[:], base[:], cst[:, C_BASE:C_BASE + E], ALU.subtract))
            dve.tensor_scalar(pad_i[:], base[:], cst[:, C_LANE:C_LANE + 1], None, ALU.add).then_inc(pad_done, 1)
            step.then(dve.tensor_tensor(nbm[:], cnt[:].unsqueeze(2).broadcast_to([P, E, 32]),
                                        cst[:, C_NUM:C_NUM + 32].unsqueeze(1).broadcast_to([P, E, 32]), ALU.is_gt))
            step.then(dve.tensor_reduce(nb[:], nbm[:], AX.X, ALU.add))
            step.then(dve.tensor_tensor(cmm[:], nb[:].unsqueeze(1).broadcast_to([P, E, E]),
                                        cst[:, C_TRI8:C_TRI8 + 64].rearrange("p (a b) -> p a b", a=E), ALU.mult))
            step.then(dve.tensor_reduce(cum[:, 0, :], cmm[:], AX.X, ALU.add))
            step.then(dve.tensor_tensor(cum[:, 1, :], cum[:, 0, :], nb[:], ALU.subtract))
            step.then(dve.scalar_tensor_tensor(org[:], cum[:, 1, :], -float(P), cst[:, C_BASE:C_BASE + E], ALU.mult, ALU.add))
            bnum = cst[:, C_BLK:C_BLK + blocks]

            def be(ap):
                return ap.unsqueeze(1).broadcast_to([P, blocks, E])

            wb = bnum.unsqueeze(2).broadcast_to([P, blocks, E])
            step.then(dve.tensor_tensor(bm[:, 0], be(cum[:, 0, :]), wb, ALU.is_le))
            step.then(dve.tensor_tensor(bm[:, 1], be(cum[:, 1, :]), wb, ALU.is_le))
            step.then(dve.tensor_tensor(bm[:, 1], bm[:, 1], bm[:, 0], ALU.subtract))
            step.then(dve.tensor_tensor(bm[:, 2], bm[:, 1], be(org[:]), ALU.mult))
            step.then(dve.tensor_reduce(br[:, 0:3], bm[:], AX.X, ALU.add))
            dve.tensor_scalar(tab[:, 1, :], br[:, 0, :], float(E - 1), None, ALU.min)
            step.then(dve.tensor_scalar(br[:, 3, :], bnum, float(P), -float(E * region), ALU.mult, ALU.add))
            step.then(dve.tensor_tensor(br[:, 3, :], br[:, 3, :], br[:, 1, :], ALU.mult))
            step.then(dve.tensor_tensor(br[:, 3, :], br[:, 3, :], br[:, 2, :], ALU.add))
            step.then(dve.tensor_scalar(tab[:, 0, :], br[:, 3, :], float(E * region), None, ALU.add))
            dve.sem_inc(tab_done, 1)

            def norm_b(b, q, turn):
                i = q % 2
                dve.wait_ge(xb_in[q], 16 * (turn + 1))
                wait(dve, xbt_done, b - 1)
                dve.tensor_scalar(xbn[i][:], xb[q][:, 0:D], xb[q][:, D:D + 1], xb[q][:, D + 1:D + 2],
                                  ALU.subtract, ALU.mult).then_inc(xbn_done, 1)

            def finish(b, q, nth):
                i = q % 2
                ex = dve.value_load(tab[0:1, 1, bass.ds(b, 1)], min_val=0, max_val=E - 1)
                dve.wait_ge(y_done, b + 1)
                wait(dve, stored[i], 16 * nth)
                dve.tensor_tensor(yo[i][:], o_ps[:, 512 * i:512 * i + D],
                                  b2_sb[:, bass.ds(ex, 1), :].rearrange("p a d -> p (a d)"), ALU.add).then_inc(yb_done, 1)
                dve.tensor_copy(tok_i[i][:], xb[q][:, D + 2:D + 3])
                dve.wait_ge(yb_done, b + 1)
                dve.scalar_tensor_tensor(yf[i][:], yo[i][:], tg[:, 1:2], xb[q][:, 0:D], ALU.mult, ALU.add).then_inc(yf_done, 1)

            dve.wait_ge(late_in, 32)
            norm_b(0, 0, 0)

            def expert_slot(b, q, turn):
                known = isinstance(b, int)
                if not known or b + 1 < blocks:
                    norm_b(b + 1, (q + 1) % 4, turn + (q + 1) // 4)
                if not known or b > 0:
                    finish(b - 1, (q - 1) % 4, 2 * turn + (q - 1) // 2)

            block_slots(dve, expert_slot, 1)

        @block.gpsimd
        def _(pool):
            def pow_x(n):
                pool.wait_ge(ln_var, n + 1)
                pool.tensor_tensor(rstd[:], ve[:], neg_half[:], ALU.pow).then_inc(ln_pow, 1)

            def pow_x1(n):
                pool.wait_ge(res_var, n + 1)
                pool.tensor_tensor(xs[:, :, D + 1], ve1[:], neg_half[:], ALU.pow).then_inc(res_pow, 1)

            def spread_v(n):
                pool.wait_ge(vt_out, n + 1)
                wait_apart(pool, av_done, 2 * n, passed_pool)
                for t in range(T8):
                    last = pool.tensor_scalar(vb[:, :, t, :], vt[:], cst[:, C_MASK + t:C_MASK + t + 1], None, ALU.mult)
                last.then_inc(vb_done, 1)

            def divide(n):
                pool.wait_ge(rt_done, n + 1)
                pool.wait_ge(om_done, 2 * n + 2)
                wait(pool, ot_done, n)
                for s in range(2):
                    last = pool.tensor_tensor(cn[:, s], om[:, s, :, 0:H],
                                              rt[:, s, 0:H].unsqueeze(1).broadcast_to([P, H, H]), ALU.mult)
                last.then_inc(cn_done, 1)

            def route(n):
                pool.wait_ge(pos_done, n + 1)
                wait_apart(pool, res_done, n + 1, passed_pool)
                for s in range(2):
                    pool.indirect_dma_start(rows, bass.IndirectOffsetOnAxis(ap=pos_i[:, s:s + 1], axis=0),
                                            xs[:, s, :], None).then_inc(routed, 16)

            def slot(k):
                if has(k, -1):
                    divide(k - 1)
                if has(k, 0):
                    spread_v(k)
                if has(k, -2):
                    route(k - 2)
                if has(k, -1):
                    pow_x1(k - 1)
                if has(k, 2):
                    pow_x(k + 2)

            pool.wait_ge(consts_ok, 1)
            pow_x(0)
            pow_x(1)
            slot(0)
            slot(1)
            with pool.Fori(2, pairs - 2) as k:
                slot(k)
            for k in range(pairs - 2, pairs + 2):
                slot(k)

            pool.wait_ge(pad_done, 1)
            for e in range(E):
                pool.indirect_dma_start(rows, bass.IndirectOffsetOnAxis(ap=pad_i[:, e:e + 1], axis=0),
                                        pad_row[:], None).then_inc(pad_in, 16)
            pool.dma_start(rows[E * region:E * region + P, :], pad_row[:]).then_inc(pad_in, 16)

            def store(b, q, turn):
                i = q % 2
                wait_apart(pool, yf_done, b + 1, passed_pool)
                pool.indirect_dma_start(out, bass.IndirectOffsetOnAxis(ap=tok_i[i][:, 0:1], axis=0),
                                        yf[i][:], None, bounds_check=tokens - 1, oob_is_err=False).then_inc(stored[i], 16)

            block_slots(pool, store, 0)


def kernel(x, ctx_1024, g_xattn, g_ffn, L0_xattn_Wq, L0_xattn_Wk, L0_xattn_Wv, L0_xattn_Wo, L0_ffn_Wg,
           L0_ffn_bg, L0_ffn_W1, L0_ffn_b1, L0_ffn_W2, L0_ffn_b2):
    import concourse.bacc as bacc
    import numpy as np
    from concourse.bass_utils import run_bass_kernel_spmd

    a = {k: np.asarray(v) for k, v in locals().items() if k in (
        "x", "ctx_1024", "g_xattn", "g_ffn", "L0_xattn_Wq", "L0_xattn_Wk", "L0_xattn_Wv", "L0_xattn_Wo",
        "L0_ffn_Wg", "L0_ffn_bg", "L0_ffn_W1", "L0_ffn_b1", "L0_ffn_W2", "L0_ffn_b2")}
    shape = a["x"].shape
    tokens = shape[0] * shape[1]
    tiles = tokens // P
    pairs = tiles // 2
    region = tokens + P
    blocks = tiles + E

    def chunked(w):
        return np.moveaxis(w.reshape(w.shape[:-2] + (KC, P, w.shape[-1])), -3, -2)

    ctx_t = a["ctx_1024"].reshape(P, pairs, 2, KC, P).transpose(1, 4, 3, 2, 0).reshape(pairs, P, KC * 2 * P)
    w_qkvo = np.stack([chunked(a[f"L0_xattn_W{n}"].T) for n in "qkvo"], axis=1)
    w1 = chunked(a["L0_ffn_W1"]).reshape(E, P, KC * D)
    b1 = a["L0_ffn_b1"].reshape(E, KC, P).transpose(0, 2, 1)
    w1b = np.concatenate([w1, b1], axis=2)
    w2 = chunked(a["L0_ffn_W2"]).transpose(1, 0, 2, 3)

    p = np.arange(P)
    consts = np.zeros((P, C_BLK + blocks), np.float32)
    consts[:, C_ID:C_ID + P] = np.eye(P)
    consts[:, C_TRI:C_TRI + P] = p[:, None] < p[None, :]
    consts[:, C_MASK:C_MASK + T8] = (p[:, None] // H) == np.arange(T8)[None, :]
    consts[:, C_REV:C_REV + E] = E - np.arange(E)
    consts[:, C_BASE:C_BASE + E] = region * np.arange(E)
    consts[:, C_TRI8:C_TRI8 + E * E] = (np.arange(E)[None, :] <= np.arange(E)[:, None]).reshape(-1)
    consts[:, C_LANE] = p
    consts[:, C_TOK:C_TOK + tiles] = tiles * p[:, None] + np.arange(tiles)[None, :]
    consts[:, C_NUM:C_NUM + 32] = P * np.arange(32)
    consts[:, C_BLK:C_BLK + blocks] = np.arange(blocks)

    ins = {
        "x_in": a["x"].reshape(tokens, D), "ctx_in": ctx_t, "gx_in": a["g_xattn"], "gf_in": a["g_ffn"],
        "wqkvo_in": w_qkvo, "wg_in": chunked(a["L0_ffn_Wg"]), "bg_in": a["L0_ffn_bg"], "w1_in_": w1b,
        "w2_in": w2, "b2_in": a["L0_ffn_b2"].reshape(-1), "consts_in": consts,
    }
    ins = {k: np.ascontiguousarray(v) for k, v in ins.items()}
    nc = bacc.Bacc("TRN2", target_bir_lowering=False, num_devices=1)
    aps = [nc.dram_tensor(k, v.shape, mybir.dt.from_np(v.dtype), kind="ExternalInput").ap() for k, v in ins.items()]
    out = nc.dram_tensor("out_rows", (tokens, D), F32, kind="ExternalOutput").ap()
    flamingo_block(nc, *aps, out)
    r = run_bass_kernel_spmd(nc, [ins], core_ids=[0])
    return r.results[0]["out_rows"].reshape(shape)
```

```python
from contextlib import ExitStack

import concourse.bass as bass
from concourse import mybir

ALU = mybir.AluOpType
ACT = mybir.ActivationFunctionType
AX = mybir.AxisListType
F32 = mybir.dt.float32
BF16 = mybir.dt.bfloat16
I32 = mybir.dt.int32
U32 = mybir.dt.uint32

P = 128
D = 256
KC = D // P
H = 16
EPS = 1e-5
GB = 4
T8 = 8
T_DVE = 4
E = 8
RING = 8
ROW = D + 4
C_ID, C_TRI, C_MASK, C_REV, C_BASE, C_TRI8 = 0, P, 2 * P, 2 * P + 8, 2 * P + 16, 2 * P + 24
C_TOK = C_TRI8 + 64
C_NUM = C_TOK + 32
C_BLK = C_NUM + 32


def wait(eng, sem, value):
    if isinstance(value, int) and value <= 0:
        return
    eng.wait_ge(sem, value)


def wait_apart(eng, sem, value, passed):
    if isinstance(value, int) and value <= 0:
        return
    eng.wait_ge(sem, value)
    eng.sem_inc(passed, 1)


class Steps:

    def __init__(self, eng, sem, call, per_call):
        self.eng, self.sem, self.base, self.per, self.at = eng, sem, call * per_call, per_call, 0

    def then(self, ins, passed=None):
        ins.then_inc(self.sem, 1)
        self.at += 1
        assert self.at <= self.per
        if passed is None:
            self.eng.wait_ge(self.sem, self.base + self.at)
        else:
            wait_apart(self.eng, self.sem, self.base + self.at, passed)


def flamingo_block(nc, x, ctx_t, g_x, g_f, w_qkvo, wg, bg, w1b, w2, b2, consts, out):
    tokens = x.shape[0]
    tiles = tokens // P
    pairs = tiles // 2
    region = tokens + P
    blocks = tiles + E
    x_v = x.rearrange("(p j) d -> p j d", p=P)
    rows = nc.dram_tensor("routed_rows", (E * region + P, ROW), F32).ap()

    with ExitStack() as stack:
        def sb(name, shape, dt=F32):
            return stack.enter_context(nc.sbuf_tensor("sb_" + name, shape, dt))

        def ps(name, shape):
            return stack.enter_context(nc.psum_tensor("ps_" + name, shape, F32))

        def sem(name):
            return stack.enter_context(nc.semaphore(name))

        cst = sb("cst", [P, C_BLK + blocks])
        wt = sb("wt", [P, 4, KC, D])
        wg_sb = sb("wg", [P, KC, E])
        bg_sb = sb("bg", [P, E])
        w2_sb = sb("w2", [P, E, KC, D])
        b2_sb = sb("b2", [P, E, D])
        gates = sb("gates", [P, 2])
        tg = sb("tg", [P, 2])
        tri = sb("tri", [P, P], BF16)
        ones = sb("ones", [P, P], BF16)
        neg_half = sb("neg_half", [P, 2])
        x_sb = sb("x", [P, tiles, D])
        ct = sb("ct", [P, KC, 2, P])
        st = sb("st", [P, 2, 6])
        mv = sb("mv", [P, 2, 2])
        ve = sb("ve", [P, 2])
        rstd = sb("rstd", [P, 2])
        xn = sb("xn", [P, 2, D])
        xt = sb("xt", [P, KC, 2, P])
        y_q = sb("y_q", [P, 32, H])
        y_k = sb("y_k", [P, 32, H])
        y_v = sb("y_v", [P, 32, H])
        qt = sb("qt", [P, 32, H])
        kt = sb("kt", [P, 32, H])
        vt = sb("vt", [P, 32, H])
        kb = sb("kb", [P, 32, T8, H])
        vb = sb("vb", [P, 32, T8, H])
        mx = sb("mx", [P, 2, 32])
        pe_x = sb("pe_x", [P, 2, 512])
        sm = sb("sm", [P, 2, 32])
        rs = sb("rs", [P, 2, 32])
        rt = sb("rt", [P, 2, 32])
        at = sb("at", [P, 2, GB, 4, H])
        om = sb("om", [P, 2, H, 32])
        cn = sb("cn", [P, 2, H, H])
        ot = sb("ot", [P, KC, 2, P])
        xs = sb("xs", [P, 2, ROW])
        st1 = sb("st1", [P, 2, 6])
        ve1 = sb("ve1", [P, 2])
        x1n = sb("x1n", [P, 2, D])
        x1t = sb("x1t", [P, KC, 2, P])
        lg = sb("lg", [P, 2, E])
        lm = sb("lm", [P, 2])
        le = sb("le", [P, 2, E])
        lw = sb("lw", [P, 2])
        oh = sb("oh", [P, 2, E])
        oh_b = sb("oh_b", [P, 2, E], BF16)
        base = sb("base", [P, E])
        rb = sb("rb", [P, 2, E])
        tot = sb("tot", [P, 2, E])
        pos = sb("pos", [P, 2])
        pos_i = sb("pos_i", [P, 2], U32)
        pad_row = sb("pad_row", [P, ROW])
        pad_i = sb("pad_i", [P, E], I32)
        cnt = sb("cnt", [P, E])
        nbm = sb("nbm", [P, E, 32])
        nb = sb("nb", [P, E])
        cmm = sb("cmm", [P, E, E])
        cum = sb("cum", [P, 2, E])
        org = sb("org", [P, E])
        bm = sb("bm", [P, 3, blocks, E])
        br = sb("br", [P, 4, blocks])
        tab = sb("tab", [P, 2, blocks], I32)
        w1_sb = [sb(f"w1_{i}", [P, KC * D + KC]) for i in range(RING)]
        xb = [sb(f"xb_{i}", [P, ROW]) for i in range(RING)]
        xbn = [sb(f"xbn_{i}", [P, D]) for i in range(2)]
        xbt = [sb(f"xbt_{i}", [P, KC, P]) for i in range(2)]
        ht = [sb(f"ht_{i}", [P, KC, P]) for i in range(2)]
        yo = [sb(f"yo_{i}", [P, D]) for i in range(2)]
        yf = [sb(f"yf_{i}", [P, D]) for i in range(2)]
        tok_i = [sb(f"tok_i_{i}", [P, 1], U32) for i in range(2)]

        tr = [ps(f"tr{i}", [P, 512]) for i in range(2)]
        pr = [ps(f"pr{i}", [P, 512]) for i in range(2)]
        s_ps = ps("s", [P, 1024])
        o_ps = ps("o", [P, 1024])

        cst_in, wt_in, gate_in, late_in = sem("cst_in"), sem("wt_in"), sem("gate_in"), sem("late_in")
        x_in, ct_in = sem("x_in"), sem("ct_in")
        setup_step, consts_ok, zero_ok = sem("setup_step"), sem("consts_ok"), sem("zero_ok")
        tanh_ok = sem("tanh_ok")
        passed_dve, passed_pool = sem("passed_dve"), sem("passed_pool")
        ln_step, ln_var, ln_pow, ln_done = sem("ln_step"), sem("ln_var"), sem("ln_pow"), sem("ln_done")
        xt_done, xt_out = sem("xt_done"), sem("xt_out")
        q_done, k_done, v_done = sem("q_done"), sem("k_done"), sem("v_done")
        yq_out, yk_out, yv_out = sem("yq_out"), sem("yk_out"), sem("yv_out")
        qt_done, kt_done, vt_done = sem("qt_done"), sem("kt_done"), sem("vt_done")
        qt_out, kt_out, vt_out = sem("qt_out"), sem("kt_out"), sem("vt_out")
        kb_done, vb_done = sem("kb_done"), sem("vb_done")
        score_done = sem("score_done")
        max_done, sub_done, exp_done = sem("max_done"), sem("sub_done"), sem("exp_done")
        at_done, at_out = sem("at_done"), sem("at_out")
        sum_done, inv_done, rt_done = sem("sum_done"), sem("inv_done"), sem("rt_done")
        av_done = sem("av_done")
        om_done = sem("om_done")
        cn_done, ot_done, ot_out, wo_done = sem("cn_done"), sem("ot_done"), sem("ot_out"), sem("wo_done")
        res_step, res_var, res_pow, res_done = sem("res_step"), sem("res_var"), sem("res_pow"), sem("res_done")
        x1t_done, x1t_out, lg_done = sem("x1t_done"), sem("x1t_out"), sem("lg_done")
        pick_step, oh_done, rank_done = sem("pick_step"), sem("oh_done"), sem("rank_done")
        pos_step, rank_read, pos_done = sem("pos_step"), sem("rank_read"), sem("pos_done")
        routed = sem("routed")
        pad_done, pad_in = sem("pad_done"), sem("pad_in")
        tab_step, tab_done = sem("tab_step"), sem("tab_done")
        xb_in = [sem(f"xb_in{i}") for i in range(RING)]
        w1_in = [sem(f"w1_in{i}") for i in range(RING)]
        xbn_done, xbt_done, xbt_out = sem("xbn_done"), sem("xbt_done"), sem("xbt_out")
        h_done, gelu_done = sem("h_done"), sem("gelu_done")
        y_done, yb_done, yf_done = sem("y_done"), sem("yb_done"), sem("yf_done")
        stored = [sem(f"stored{i}") for i in range(2)]

        ident = cst[:, C_ID:C_ID + P]
        block = stack.enter_context(nc.Block())

        def slots(eng, pre, slot):
            pre()
            slot(0)
            slot(1)
            with eng.Fori(2, pairs - 1) as k:
                slot(k)
            slot(pairs - 1)
            slot(pairs)
            slot(pairs + 1)

        def has(k, shift):
            return not isinstance(k, int) or 0 <= k + shift < pairs

        def block_slots(eng, slot, skew):
            for b in range(RING):
                slot(b, b, 0)
            with eng.Fori(1, blocks // RING - 1) as turn:
                for q in range(RING):
                    slot(RING * turn + q, q, turn)
            for b in range(blocks - RING, blocks + skew):
                slot(b, b % RING, b // RING)

        @block.sync
        def _(sp):
            def pre():
                sp.dma_start(cst[:], consts).then_inc(cst_in, 16)
                sp.dma_start(x_sb[:, 0:2, :], x_v[:, 0:2, :]).then_inc(x_in, 16)
                sp.dma_start(ct[:].rearrange("p a b c -> p (a b c)"), ctx_t[0]).then_inc(ct_in, 16)
                sp.dma_start(wt[:], w_qkvo).then_inc(wt_in, 16)
                sp.dma_start(gates[:, 0:1], g_x.partition_broadcast(P)).then_inc(gate_in, 16)
                sp.dma_start(gates[:, 1:2], g_f.partition_broadcast(P)).then_inc(gate_in, 16)
                sp.dma_start(wg_sb[:], wg).then_inc(gate_in, 16)
                sp.dma_start(bg_sb[:], bg.partition_broadcast(P)).then_inc(gate_in, 16)

            def load(n):
                sp.wait_ge(x_in, 16 * n)
                sp.dma_start(x_sb[:, bass.ds(2 * n, 2), :], x_v[:, bass.ds(2 * n, 2), :]).then_inc(x_in, 16)
                sp.wait_ge(v_done, n)
                sp.dma_start(ct[:].rearrange("p a b c -> p (a b c)"),
                             ctx_t[bass.ds(n, 1)].rearrange("a p f -> p (a f)")).then_inc(ct_in, 16)

            pre()
            load(1)
            sp.wait_ge(consts_ok, 1)
            sp.dma_start(rows[E * region:E * region + P, :], pad_row[:]).then_inc(pad_in, 16)
            sp.dma_start(w2_sb[:], w2).then_inc(late_in, 16)
            sp.dma_start(b2_sb[:].rearrange("p e d -> p (e d)"), b2.partition_broadcast(P)).then_inc(late_in, 16)
            with sp.Fori(2, pairs) as n:
                load(n)

            sp.wait_ge(pad_done, 1)
            for e in range(E):
                row = sp.value_load(pad_i[0:1, e:e + 1], min_val=0, max_val=E * region)
                sp.dma_start(rows[bass.ds(row, P), :], pad_row[:]).then_inc(pad_in, 16)
            sp.wait_ge(tab_done, 1)
            sp.wait_ge(routed, 32 * pairs)
            sp.wait_ge(pad_in, 16 * (E + 1))

            def fetch(b, q, turn):
                row = sp.value_load(tab[0:1, 0, bass.ds(b, 1)], min_val=0, max_val=E * region)
                ex = sp.value_load(tab[0:1, 1, bass.ds(b, 1)], min_val=0, max_val=E - 1)
                wait(sp, yf_done, b - RING + 1)
                sp.dma_start(xb[q][:], rows[bass.ds(row, P), :]).then_inc(xb_in[q], 16)
                wait(sp, gelu_done, b - RING + 1)
                sp.dma_start(w1_sb[q][:], w1b[bass.ds(ex, 1)].rearrange("a p f -> p (a f)")).then_inc(w1_in[q], 16)

            block_slots(sp, fetch, 0)
            for i in range(2):
                sp.wait_ge(stored[i], 8 * blocks)

        @block.tensor
        def _(pe):
            def transpose_x(n):
                pe.wait_ge(ln_done, n + 1)
                wait(pe, qt_out, n)
                for kc in range(KC):
                    for s in range(2):
                        q = (kc * 2 + s) * P
                        last = pe.transpose(tr[0][:, q:q + P], xn[:, s, kc * P:(kc + 1) * P], ident)
                last.then_inc(xt_done, 1)

            def project(src, w, bank, done):
                for s in range(2):
                    for kc in range(KC):
                        last = pe.matmul(pr[bank][:, s * D:(s + 1) * D], lhsT=src[:, kc, s, :],
                                         rhs=wt[:, w, kc, :], start=(kc == 0), stop=(kc == KC - 1))
                last.then_inc(done, 1)

            def project_k(n):
                pe.wait_ge(ct_in, 16 * (n + 1))
                wait(pe, yq_out, n)
                wait(pe, oh_done, n - 2)
                project(ct, 1, 1, k_done)

            def project_v(n):
                wait(pe, yv_out, n)
                wait(pe, rank_read, n - 2)
                project(ct, 2, 0, v_done)

            def project_q(n):
                pe.wait_ge(xt_out, n + 1)
                pe.wait_ge(yk_out, n + 1)
                project(xt, 0, 1, q_done)

            def transpose_y(y, bank, done):
                for g in range(GB):
                    last = pe.transpose(tr[bank][:, g * P:(g + 1) * P],
                                        y[:, T8 * g:T8 * (g + 1), :].rearrange("p t h -> p (t h)"), ident)
                last.then_inc(done, 1)

            def transpose_k(n):
                pe.wait_ge(yk_out, n + 1)
                pe.wait_ge(xt_out, n + 1)
                transpose_y(y_k, 0, kt_done)

            def transpose_v(n):
                pe.wait_ge(yv_out, n + 1)
                wait(pe, vt_out, n)
                wait(pe, ot_out, n - 1)
                transpose_y(y_v, 1, vt_done)

            def transpose_q(n):
                pe.wait_ge(yq_out, n + 1)
                pe.wait_ge(kt_out, n + 1)
                wait(pe, at_out, 2 * n - 1)
                transpose_y(y_q, 0, qt_done)

            def scores(n):
                pe.wait_ge(qt_out, n + 1)
                pe.wait_ge(kb_done, 2 * n + 2)
                wait(pe, sub_done, 2 * n)
                if isinstance(n, int) and n == 0:
                    pe.wait_ge(zero_ok, 1)
                for s in range(2):
                    for g in range(GB):
                        for c in range(4):
                            i = (g * 4 + c) * 2 + s
                            q = s * 512 + g * P
                            last = pe.matmul(s_ps[32 * c:32 * c + H, q:q + P], lhsT=qt[:, i, :],
                                             rhs=kb[:, i, :, :].rearrange("p t j -> p (t j)"),
                                             start=True, stop=True)
                    last.then_inc(score_done, 1)

            def transpose_a(n, more):
                for s in range(2):
                    pe.wait_ge(exp_done, 2 * n + s + 1)
                    if more:
                        pe.wait_ge((kt_out, vt_out)[s], n + 2)
                    elif s == 1:
                        pe.wait_ge(ot_out, n)
                    for g in range(GB):
                        last = pe.transpose(tr[s][:, g * P:(g + 1) * P],
                                            pe_x[:, s, g * P:(g + 1) * P], ident)
                    last.then_inc(at_done, 1)

            def values(n):
                pe.wait_ge(vb_done, n + 1)
                wait(pe, om_done, 2 * n)
                for s in range(2):
                    pe.wait_ge(at_out, 2 * n + s + 1)
                    for g in range(GB):
                        for c in range(4):
                            i = (g * 4 + c) * 2 + s
                            q = s * 512 + g * P
                            last = pe.matmul(o_ps[32 * c:32 * c + H, q:q + P], lhsT=at[:, s, g, c, :],
                                             rhs=vb[:, i, :, :].rearrange("p t h -> p (t h)"),
                                             start=True, stop=True)
                    last.then_inc(av_done, 1)

            def transpose_o(n):
                pe.wait_ge(cn_done, n + 1)
                wait(pe, x1t_out, n)
                for kc in range(KC):
                    for s in range(2):
                        q = (kc * 2 + s) * P
                        last = pe.transpose(tr[1][:, q:q + P],
                                            cn[:, s, 8 * kc:8 * kc + 8, :].rearrange("p h i -> p (h i)"), ident)
                last.then_inc(ot_done, 1)

            def project_o(n, more):
                pe.wait_ge(ot_out, n + 1)
                if more:
                    pe.wait_ge(yv_out, n + 3)
                wait(pe, rank_read, n)
                project(ot, 3, 0, wo_done)

            def transpose_x1(n, halves):
                pe.wait_ge(res_done, n + 1)
                pe.wait_ge(at_out, halves)
                for kc in range(KC):
                    for s in range(2):
                        q = (kc * 2 + s) * P
                        last = pe.transpose(tr[1][:, q:q + P], x1n[:, s, kc * P:(kc + 1) * P], ident)
                last.then_inc(x1t_done, 1)

            def logits(n, more):
                pe.wait_ge(x1t_out, n + 1)
                if more:
                    pe.wait_ge(yq_out, n + 3)
                wait(pe, oh_done, n)
                for s in range(2):
                    for kc in range(KC):
                        last = pe.matmul(pr[1][:, s * E:(s + 1) * E], lhsT=x1t[:, kc, s, :],
                                         rhs=wg_sb[:, kc, :], start=(kc == 0), stop=(kc == KC - 1))
                last.then_inc(lg_done, 1)

            def ranks(n):
                pe.wait_ge(oh_done, n + 1)
                rhs = oh_b[:].rearrange("p s e -> p (s e)")
                pe.matmul(pr[0][:, 0:2 * E], lhsT=tri[:], rhs=rhs, start=True, stop=True)
                pe.matmul(pr[0][:, 2 * E:4 * E], lhsT=ones[:], rhs=rhs, start=True, stop=True).then_inc(rank_done, 1)

            def slot(k):
                more = has(k, 1)
                if has(k, 0):
                    scores(k)
                if has(k, -2):
                    ranks(k - 2)
                if more:
                    transpose_x(k + 1)
                    project_k(k + 1)
                if has(k, -1):
                    transpose_o(k - 1)
                if more:
                    project_v(k + 1)
                    transpose_k(k + 1)
                    project_q(k + 1)
                    transpose_v(k + 1)
                if has(k, -1):
                    project_o(k - 1, more)
                if has(k, 0):
                    transpose_a(k, more)
                if more:
                    transpose_q(k + 1)
                if has(k, 0):
                    values(k)
                if has(k, -1):
                    transpose_x1(k - 1, 2 * k + 2 if has(k, 0) else 2 * pairs)
                    logits(k - 1, more)

            def pre():
                pe.wait_ge(cst_in, 16)
                transpose_x(0)
                pe.wait_ge(wt_in, 16)
                project_k(0)
                project_v(0)
                transpose_k(0)
                project_q(0)
                transpose_v(0)
                transpose_q(0)
                pe.wait_ge(gate_in, 64)
                pe.wait_ge(consts_ok, 1)

            slots(pe, pre, slot)

            def transpose_b(b, i):
                pe.wait_ge(xbn_done, b + 1)
                wait(pe, xbt_out, b - 1)
                for kc in range(KC):
                    last = pe.transpose(tr[i][:, kc * P:(kc + 1) * P], xbn[i][:, kc * P:(kc + 1) * P], ident)
                last.then_inc(xbt_done, 1)

            def layer1(b, q, turn):
                i = q % 2
                pe.wait_ge(xbt_out, b + 1)
                pe.wait_ge(w1_in[q], 16 * (turn + 1))
                wait(pe, gelu_done, b - 1)
                for ic in range(KC):
                    for kc in range(KC):
                        last = pe.matmul(pr[i][:, ic * P:(ic + 1) * P],
                                         lhsT=w1_sb[q][:, kc * D + ic * P:kc * D + (ic + 1) * P],
                                         rhs=xbt[i][:, kc, :], start=(kc == 0), stop=(kc == KC - 1))
                last.then_inc(h_done, 1)

            def layer2(b, i):
                ex = pe.value_load(tab[0:1, 1, bass.ds(b, 1)], min_val=0, max_val=E - 1)
                pe.wait_ge(gelu_done, b + 1)
                wait(pe, yb_done, b - 1)
                for ic in range(KC):
                    last = pe.matmul(o_ps[:, 512 * i:512 * i + D], lhsT=ht[i][:, ic, :],
                                     rhs=w2_sb[:, bass.ds(ex, 1), ic, :].rearrange("p a d -> p (a d)"),
                                     start=(ic == 0), stop=(ic == KC - 1))
                last.then_inc(y_done, 1)

            pe.wait_ge(late_in, 32)
            pe.wait_ge(tab_done, 1)
            transpose_b(0, 0)
            transpose_b(1, 1)

            def expert_slot(b, q, turn):
                i = q % 2
                known = isinstance(b, int)
                if not known or b < blocks:
                    layer1(b, q, turn)
                if not known or b > 0:
                    layer2(b - 1, 1 - i)
                if not known or b + 2 < blocks:
                    transpose_b(b + 2, i)

            block_slots(pe, expert_slot, 1)

        @block.scalar
        def _(act):
            def copy_xt(n):
                act.wait_ge(xt_done, n + 1)
                wait(act, q_done, n)
                act.copy(xt[:].rearrange("p a b c -> p (a b c)"), tr[0][:]).then_inc(xt_out, 1)

            def copy_qt(n):
                act.wait_ge(qt_done, n + 1)
                wait(act, score_done, 2 * n)
                act.copy(qt[:].rearrange("p a b -> p (a b)"), tr[0][:]).then_inc(qt_out, 1)

            def copy_kt(n):
                act.wait_ge(kt_done, n + 1)
                wait(act, kb_done, 2 * n)
                act.copy(kt[:].rearrange("p a b -> p (a b)"), tr[0][:]).then_inc(kt_out, 1)

            def copy_vt(n):
                act.wait_ge(vt_done, n + 1)
                wait(act, vb_done, n)
                act.copy(vt[:].rearrange("p a b -> p (a b)"), tr[1][:]).then_inc(vt_out, 1)

            def spread(dst, src, first):
                for t in range(first, T8):
                    last = act.activation(dst[:, :, t, :], src[:], ACT.Copy, scale=cst[:, C_MASK + t:C_MASK + t + 1])
                return last

            def spread_k(n):
                wait(act, score_done, 2 * n)
                act.wait_ge(kt_out, n + 1)
                spread(kb, kt, T_DVE).then_inc(kb_done, 1)

            def spread_v(n):
                wait(act, av_done, 2 * n)
                act.wait_ge(vt_out, n + 1)
                spread(vb, vt, 0).then_inc(vb_done, 1)

            def exps(n, s):
                act.wait_ge(sub_done, 2 * n + s + 1)
                act.activation(pe_x[:, s, :], pe_x[:, s, :], ACT.Exp, scale=float(H) ** -0.5).then_inc(exp_done, 1)

            def copy_at(n, s):
                act.wait_ge(at_done, 2 * n + s + 1)
                wait(act, av_done, 2 * n)
                act.copy(at[:, s].rearrange("p g c i -> p (g c) i"),
                         tr[s][:].rearrange("p (q w) -> p q w", w=32)[:, :, 0:H]).then_inc(at_out, 1)

            def copy_ot(n):
                act.wait_ge(ot_done, n + 1)
                wait(act, wo_done, n)
                act.copy(ot[:].rearrange("p a b c -> p (a b c)"), tr[1][:]).then_inc(ot_out, 1)

            def copy_x1t(n):
                act.wait_ge(x1t_done, n + 1)
                wait(act, lg_done, n)
                act.copy(x1t[:].rearrange("p a b c -> p (a b c)"), tr[1][:]).then_inc(x1t_out, 1)

            def slot(k):
                more = has(k, 1)
                if has(k, 0):
                    spread_v(k)
                if more:
                    copy_xt(k + 1)
                if has(k, 0):
                    exps(k, 0)
                if has(k, -1):
                    copy_ot(k - 1)
                if has(k, 0):
                    exps(k, 1)
                if more:
                    copy_kt(k + 1)
                    spread_k(k + 1)
                    copy_vt(k + 1)
                if has(k, 0):
                    copy_at(k, 0)
                    copy_at(k, 1)
                if more:
                    copy_qt(k + 1)
                if has(k, -1):
                    copy_x1t(k - 1)

            def pre():
                act.wait_ge(gate_in, 64)
                act.activation(tg[:], gates[:], ACT.Tanh).then_inc(tanh_ok, 1)
                copy_xt(0)
                copy_kt(0)
                spread_k(0)
                copy_vt(0)
                copy_qt(0)

            slots(act, pre, slot)

            def expert_slot(b, q, turn):
                i = q % 2
                known = isinstance(b, int)
                if not known or b < blocks:
                    act.wait_ge(h_done, b + 1)
                    wait(act, y_done, b - 1)
                    for ic in range(KC):
                        last = act.activation(ht[i][:, ic, :], pr[i][:, ic * P:(ic + 1) * P], ACT.Gelu,
                                              bias=w1_sb[q][:, KC * D + ic:KC * D + ic + 1])
                    last.then_inc(gelu_done, 1)
                if not known or b + 2 < blocks:
                    copy_xbt(b + 2, i)

            def copy_xbt(b, i):
                act.wait_ge(xbt_done, b + 1)
                wait(act, h_done, b - 1)
                act.copy(xbt[i][:].rearrange("p a b -> p (a b)"), tr[i][:, 0:KC * P]).then_inc(xbt_out, 1)

            copy_xbt(0, 0)
            copy_xbt(1, 1)
            block_slots(act, expert_slot, 0)

        @block.vector
        def _(dve):
            def stats_x(n):
                step = Steps(dve, ln_step, n, 2)
                dve.wait_ge(x_in, 16 * (n + 1))
                for s in range(2):
                    last = dve.bn_stats(st[:, s, :], x_sb[:, bass.ds(2 * n + s, 1), :].rearrange("p a d -> p (a d)"))
                step.then(last, passed_dve)
                for s in range(2):
                    last = dve.bn_aggr(mv[:, s, :], st[:, s, :])
                step.then(last)
                dve.tensor_scalar(ve[:], mv[:, :, 1], EPS, None, ALU.add).then_inc(ln_var, 1)

            def norm_x(n):
                dve.wait_ge(ln_pow, n + 1)
                wait(dve, xt_done, n)
                for s in range(2):
                    last = dve.tensor_scalar(xn[:, s, :], x_sb[:, bass.ds(2 * n + s, 1), :].rearrange("p a d -> p (a d)"),
                                             mv[:, s, 0:1], rstd[:, s:s + 1], ALU.subtract, ALU.mult)
                last.then_inc(ln_done, 1)

            def turn_qk(n, done, done_t, y, bank, out_sem):
                dve.wait_ge(done, n + 1)
                wait(dve, done_t, n)
                dve.transpose(y[:].rearrange("p t h -> p h t"),
                              pr[bank][:].rearrange("p (s h i) -> p h s i", s=2, h=H)).then_inc(out_sem, 1)

            def turn_v(n):
                dve.wait_ge(v_done, n + 1)
                wait(dve, vt_done, n)
                dve.transpose(y_v[:].rearrange("p t j -> p j t"),
                              pr[0][:].rearrange("p (s h j) -> p j s h", s=2, h=H)).then_inc(yv_out, 1)

            def spread_k(n):
                dve.wait_ge(kt_out, n + 1)
                wait(dve, score_done, 2 * n)
                for t in range(T_DVE):
                    last = dve.tensor_scalar(kb[:, :, t, :], kt[:], cst[:, C_MASK + t:C_MASK + t + 1], None, ALU.mult)
                last.then_inc(kb_done, 1)

            def shift(n, s):
                dve.wait_ge(score_done, 2 * n + s + 1)
                sv = s_ps[:, 512 * s:512 * (s + 1)].rearrange("p (t j) -> p t j", j=H)
                dve.tensor_reduce(mx[:, s, :], sv, AX.X, ALU.max).then_inc(max_done, 1)
                wait(dve, at_done, 2 * n)
                dve.wait_ge(max_done, 2 * n + s + 1)
                dve.tensor_tensor(pe_x[:, s, :].rearrange("p (t j) -> p t j", j=H), sv,
                                  mx[:, s, :].unsqueeze(2).broadcast_to([P, 32, H]), ALU.subtract).then_inc(sub_done, 1)

            def sums(n, s):
                dve.wait_ge(exp_done, 2 * n + s + 1)
                dve.tensor_reduce(sm[:, s, :], pe_x[:, s, :].rearrange("p (t j) -> p t j", j=H), AX.X, ALU.add).then_inc(sum_done, 1)

            def invert(n):
                dve.wait_ge(sum_done, 2 * n + 2)
                dve.reciprocal(rs[:], sm[:]).then_inc(inv_done, 1)
                dve.wait_ge(inv_done, n + 1)
                wait(dve, cn_done, n)
                dve.transpose(rt[:].rearrange("p s t -> p (s t)"), rs[:].rearrange("p s t -> p (s t)")).then_inc(rt_done, 1)

            def turn_o(n):
                wait(dve, cn_done, n)
                for s in range(2):
                    dve.wait_ge(av_done, 2 * n + s + 1)
                    dve.transpose(om[:, s], o_ps[:, 512 * s:512 * (s + 1)].rearrange("p (t h) -> p h t", h=H)).then_inc(om_done, 1)

            def residual(n):
                step = Steps(dve, res_step, n, 3)
                dve.wait_ge(wo_done, n + 1)
                wait(dve, routed, 32 * n)
                step.then(dve.scalar_tensor_tensor(xs[:, :, 0:D], pr[0][:].rearrange("p (s d) -> p s d", s=2), tg[:, 0:1],
                                                   x_sb[:, bass.ds(2 * n, 2), :], ALU.mult, ALU.add))
                for s in range(2):
                    last = dve.bn_stats(st1[:, s, :], xs[:, s, 0:D])
                step.then(last, passed_dve)
                for s in range(2):
                    last = dve.bn_aggr(xs[:, s, D:D + 2], st1[:, s, :])
                step.then(last)
                dve.tensor_scalar(ve1[:], xs[:, :, D + 1], EPS, None, ALU.add).then_inc(res_var, 1)
                dve.tensor_copy(xs[:, :, D + 2], cst[:, bass.ds(C_TOK + 2 * n, 2)])

            def norm_x1(n):
                dve.wait_ge(res_pow, n + 1)
                wait(dve, x1t_done, n)
                for s in range(2):
                    last = dve.tensor_scalar(x1n[:, s, :], xs[:, s, 0:D], xs[:, s, D:D + 1], xs[:, s, D + 1:D + 2],
                                             ALU.subtract, ALU.mult)
                last.then_inc(res_done, 1)

            def wide(ap):
                return ap.unsqueeze(1).broadcast_to([P, 2, E])

            def deep(ap):
                return ap.unsqueeze(2).broadcast_to([P, 2, E])

            def pick(n):
                step = Steps(dve, pick_step, n, 5)
                dve.wait_ge(lg_done, n + 1)
                step.then(dve.tensor_tensor(lg[:], pr[1][:, 0:2 * E].rearrange("p (s e) -> p s e", s=2), wide(bg_sb[:]), ALU.add))
                step.then(dve.tensor_reduce(lm[:], lg[:], AX.X, ALU.max))
                step.then(dve.tensor_tensor(lg[:], lg[:], deep(lm[:]), ALU.is_equal))
                step.then(dve.tensor_tensor(le[:], lg[:], wide(cst[:, C_REV:C_REV + E]), ALU.mult))
                step.then(dve.tensor_reduce(lw[:], le[:], AX.X, ALU.max))
                wait(dve, rank_done, n)
                dve.tensor_tensor(oh[:], le[:], deep(lw[:]), ALU.is_equal)
                dve.tensor_tensor(oh_b[:], le[:], deep(lw[:]), ALU.is_equal).then_inc(oh_done, 1)

            def place(n):
                step = Steps(dve, pos_step, n, 6)
                dve.wait_ge(rank_done, n + 1)
                dve.tensor_copy(tot[:].rearrange("p s e -> p (s e)"), pr[0][:, 2 * E:4 * E])
                step.then(dve.tensor_tensor(rb[:], pr[0][:, 0:2 * E].rearrange("p (s e) -> p s e", s=2), wide(base[:]), ALU.add))
                dve.sem_inc(rank_read, 1)
                step.then(dve.tensor_tensor(rb[:, 1, :], rb[:, 1, :], tot[:, 0, :], ALU.add))
                step.then(dve.tensor_tensor(rb[:], rb[:], oh[:], ALU.mult))
                step.then(dve.tensor_reduce(pos[:], rb[:], AX.X, ALU.add))
                dve.tensor_copy(pos_i[:], pos[:]).then_inc(pos_done, 1)
                step.then(dve.tensor_tensor(base[:], base[:], tot[:, 0, :], ALU.add))
                step.then(dve.tensor_tensor(base[:], base[:], tot[:, 1, :], ALU.add))

            def slot(k):
                more = has(k, 1)
                if has(k, 2):
                    stats_x(k + 2)
                if has(k, 0):
                    shift(k, 0)
                    shift(k, 1)
                if has(k, -2):
                    place(k - 2)
                if more:
                    turn_qk(k + 1, k_done, kt_done, y_k, 1, yk_out)
                if has(k, 2):
                    norm_x(k + 2)
                if has(k, 0):
                    sums(k, 0)
                if more:
                    turn_v(k + 1)
                if has(k, 0):
                    sums(k, 1)
                    invert(k)
                if more:
                    turn_qk(k + 1, q_done, qt_done, y_q, 1, yq_out)
                    spread_k(k + 1)
                if has(k, -1):
                    residual(k - 1)
                    norm_x1(k - 1)
                if has(k, 0):
                    turn_o(k)
                if has(k, -1):
                    pick(k - 1)

            def pre():
                step = Steps(dve, setup_step, 0, 2)
                dve.memset(neg_half[:], -0.5)
                dve.memset(xs[:], 0.0)
                dve.memset(ones[:], 1.0)
                dve.memset(pad_row[:], 0.0)
                dve.memset(s_ps[:], 0.0)
                step.then(dve.memset(o_ps[:], 0.0))
                dve.memset(pad_row[:, D + 2:D + 3], 2.0 * tokens)
                dve.wait_ge(cst_in, 16)
                dve.tensor_copy(tri[:], cst[:, C_TRI:C_TRI + P])
                step.then(dve.tensor_copy(base[:], cst[:, C_BASE:C_BASE + E]))
                dve.sem_inc(zero_ok, 1)
                dve.sem_inc(consts_ok, 1)
                stats_x(0)
                norm_x(0)
                turn_qk(0, k_done, kt_done, y_k, 1, yk_out)
                turn_v(0)
                turn_qk(0, q_done, qt_done, y_q, 1, yq_out)
                stats_x(1)
                norm_x(1)
                spread_k(0)
                dve.wait_ge(gate_in, 64)
                dve.wait_ge(tanh_ok, 1)

            pre()
            slot(0)
            slot(1)
            with dve.Fori(2, pairs - 2) as k:
                slot(k)
            for k in range(pairs - 2, pairs + 2):
                slot(k)

            step = Steps(dve, tab_step, 0, 17)
            step.then(dve.tensor_tensor(cnt[:], base[:], cst[:, C_BASE:C_BASE + E], ALU.subtract))
            dve.tensor_copy(pad_i[:], base[:]).then_inc(pad_done, 1)
            step.then(dve.tensor_tensor(nbm[:], cnt[:].unsqueeze(2).broadcast_to([P, E, 32]),
                                        cst[:, C_NUM:C_NUM + 32].unsqueeze(1).broadcast_to([P, E, 32]), ALU.is_gt))
            step.then(dve.tensor_reduce(nb[:], nbm[:], AX.X, ALU.add))
            step.then(dve.tensor_tensor(cmm[:], nb[:].unsqueeze(1).broadcast_to([P, E, E]),
                                        cst[:, C_TRI8:C_TRI8 + 64].rearrange("p (a b) -> p a b", a=E), ALU.mult))
            step.then(dve.tensor_reduce(cum[:, 0, :], cmm[:], AX.X, ALU.add))
            step.then(dve.tensor_tensor(cum[:, 1, :], cum[:, 0, :], nb[:], ALU.subtract))
            step.then(dve.scalar_tensor_tensor(org[:], cum[:, 1, :], -float(P), cst[:, C_BASE:C_BASE + E], ALU.mult, ALU.add))
            bnum = cst[:, C_BLK:C_BLK + blocks]

            def be(ap):
                return ap.unsqueeze(1).broadcast_to([P, blocks, E])

            wb = bnum.unsqueeze(2).broadcast_to([P, blocks, E])
            step.then(dve.tensor_tensor(bm[:, 0], be(cum[:, 0, :]), wb, ALU.is_le))
            step.then(dve.tensor_tensor(bm[:, 1], be(cum[:, 1, :]), wb, ALU.is_le))
            step.then(dve.tensor_tensor(bm[:, 1], bm[:, 1], bm[:, 0], ALU.subtract))
            step.then(dve.tensor_tensor(bm[:, 2], bm[:, 1], be(org[:]), ALU.mult))
            step.then(dve.tensor_reduce(br[:, 0:3], bm[:], AX.X, ALU.add))
            dve.tensor_scalar(tab[:, 1, :], br[:, 0, :], float(E - 1), None, ALU.min)
            step.then(dve.tensor_scalar(br[:, 3, :], bnum, float(P), -float(E * region), ALU.mult, ALU.add))
            step.then(dve.tensor_tensor(br[:, 3, :], br[:, 3, :], br[:, 1, :], ALU.mult))
            step.then(dve.tensor_tensor(br[:, 3, :], br[:, 3, :], br[:, 2, :], ALU.add))
            step.then(dve.tensor_scalar(tab[:, 0, :], br[:, 3, :], float(E * region), None, ALU.add))
            dve.sem_inc(tab_done, 1)

            def norm_b(b, q, turn):
                i = q % 2
                dve.wait_ge(xb_in[q], 16 * (turn + 1))
                wait(dve, xbt_done, b - 1)
                dve.tensor_scalar(xbn[i][:], xb[q][:, 0:D], xb[q][:, D:D + 1], xb[q][:, D + 1:D + 2],
                                  ALU.subtract, ALU.mult).then_inc(xbn_done, 1)

            def finish(b, q, nth):
                i = q % 2
                ex = dve.value_load(tab[0:1, 1, bass.ds(b, 1)], min_val=0, max_val=E - 1)
                dve.wait_ge(y_done, b + 1)
                wait(dve, stored[i], 16 * nth)
                dve.tensor_tensor(yo[i][:], o_ps[:, 512 * i:512 * i + D],
                                  b2_sb[:, bass.ds(ex, 1), :].rearrange("p a d -> p (a d)"), ALU.add).then_inc(yb_done, 1)
                dve.tensor_copy(tok_i[i][:], xb[q][:, D + 2:D + 3])
                dve.wait_ge(yb_done, b + 1)
                dve.scalar_tensor_tensor(yf[i][:], yo[i][:], tg[:, 1:2], xb[q][:, 0:D], ALU.mult, ALU.add).then_inc(yf_done, 1)

            dve.wait_ge(late_in, 32)
            for b in range(3):
                norm_b(b, b, 0)

            def expert_slot(b, q, turn):
                known = isinstance(b, int)
                if not known or b + 3 < blocks:
                    norm_b(b + 3, (q + 3) % RING, turn + (q + 3) // RING)
                if not known or b > 0:
                    finish(b - 1, (q - 1) % RING, RING // 2 * turn + (q - 1) // 2)

            block_slots(dve, expert_slot, 1)

        @block.gpsimd
        def _(pool):
            def pow_x(n):
                pool.wait_ge(ln_var, n + 1)
                pool.tensor_tensor(rstd[:], ve[:], neg_half[:], ALU.pow).then_inc(ln_pow, 1)

            def pow_x1(n):
                pool.wait_ge(res_var, n + 1)
                pool.tensor_tensor(xs[:, :, D + 1], ve1[:], neg_half[:], ALU.pow).then_inc(res_pow, 1)

            def divide(n):
                pool.wait_ge(rt_done, n + 1)
                pool.wait_ge(om_done, 2 * n + 2)
                wait(pool, ot_done, n)
                for s in range(2):
                    last = pool.tensor_tensor(cn[:, s], om[:, s, :, 0:H],
                                              rt[:, s, 0:H].unsqueeze(1).broadcast_to([P, H, H]), ALU.mult)
                last.then_inc(cn_done, 1)

            def route(n):
                pool.wait_ge(pos_done, n + 1)
                wait_apart(pool, res_done, n + 1, passed_pool)
                for s in range(2):
                    pool.indirect_dma_start(rows, bass.IndirectOffsetOnAxis(ap=pos_i[:, s:s + 1], axis=0),
                                            xs[:, s, :], None).then_inc(routed, 16)

            def slot(k):
                if has(k, 2):
                    pow_x(k + 2)
                if has(k, -1):
                    divide(k - 1)
                if has(k, -2):
                    route(k - 2)
                if has(k, -1):
                    pow_x1(k - 1)

            pool.wait_ge(consts_ok, 1)
            pow_x(0)
            pow_x(1)
            slot(0)
            slot(1)
            with pool.Fori(2, pairs - 2) as k:
                slot(k)
            for k in range(pairs - 2, pairs + 2):
                slot(k)

            def store(b, q, turn):
                i = q % 2
                wait_apart(pool, yf_done, b + 1, passed_pool)
                pool.indirect_dma_start(out, bass.IndirectOffsetOnAxis(ap=tok_i[i][:, 0:1], axis=0),
                                        yf[i][:], None, bounds_check=tokens - 1, oob_is_err=False).then_inc(stored[i], 16)

            block_slots(pool, store, 0)


def kernel(x, ctx_1024, g_xattn, g_ffn, L0_xattn_Wq, L0_xattn_Wk, L0_xattn_Wv, L0_xattn_Wo, L0_ffn_Wg,
           L0_ffn_bg, L0_ffn_W1, L0_ffn_b1, L0_ffn_W2, L0_ffn_b2):
    import concourse.bacc as bacc
    import numpy as np
    from concourse.bass_utils import run_bass_kernel_spmd

    a = {k: np.asarray(v) for k, v in locals().items() if k in (
        "x", "ctx_1024", "g_xattn", "g_ffn", "L0_xattn_Wq", "L0_xattn_Wk", "L0_xattn_Wv", "L0_xattn_Wo",
        "L0_ffn_Wg", "L0_ffn_bg", "L0_ffn_W1", "L0_ffn_b1", "L0_ffn_W2", "L0_ffn_b2")}
    shape = a["x"].shape
    tokens = shape[0] * shape[1]
    tiles = tokens // P
    pairs = tiles // 2
    region = tokens + P
    blocks = tiles + E

    def chunked(w):
        return np.moveaxis(w.reshape(w.shape[:-2] + (KC, P, w.shape[-1])), -3, -2)

    ctx_t = a["ctx_1024"].reshape(P, pairs, 2, KC, P).transpose(1, 4, 3, 2, 0).reshape(pairs, P, KC * 2 * P)
    w_qkvo = np.stack([chunked(a[f"L0_xattn_W{n}"].T) for n in "qkvo"], axis=1)
    w1 = chunked(a["L0_ffn_W1"]).reshape(E, P, KC * D)
    b1 = a["L0_ffn_b1"].reshape(E, KC, P).transpose(0, 2, 1)
    w1b = np.concatenate([w1, b1], axis=2)
    w2 = chunked(a["L0_ffn_W2"]).transpose(1, 0, 2, 3)

    p = np.arange(P)
    consts = np.zeros((P, C_BLK + blocks), np.float32)
    consts[:, C_ID:C_ID + P] = np.eye(P)
    consts[:, C_TRI:C_TRI + P] = p[:, None] < p[None, :]
    consts[:, C_MASK:C_MASK + T8] = (p[:, None] // H) == np.arange(T8)[None, :]
    consts[:, C_REV:C_REV + E] = E - np.arange(E)
    consts[:, C_BASE:C_BASE + E] = region * np.arange(E)
    consts[:, C_TRI8:C_TRI8 + E * E] = (np.arange(E)[None, :] <= np.arange(E)[:, None]).reshape(-1)
    consts[:, C_TOK:C_TOK + tiles] = tiles * p[:, None] + np.arange(tiles)[None, :]
    consts[:, C_NUM:C_NUM + 32] = P * np.arange(32)
    consts[:, C_BLK:C_BLK + blocks] = np.arange(blocks)

    ins = {
        "x_in": a["x"].reshape(tokens, D), "ctx_in": ctx_t, "gx_in": a["g_xattn"], "gf_in": a["g_ffn"],
        "wqkvo_in": w_qkvo, "wg_in": chunked(a["L0_ffn_Wg"]), "bg_in": a["L0_ffn_bg"], "w1_in_": w1b,
        "w2_in": w2, "b2_in": a["L0_ffn_b2"].reshape(-1), "consts_in": consts,
    }
    ins = {k: np.ascontiguousarray(v) for k, v in ins.items()}
    nc = bacc.Bacc("TRN2", target_bir_lowering=False, num_devices=1)
    aps = [nc.dram_tensor(k, v.shape, mybir.dt.from_np(v.dtype), kind="ExternalInput").ap() for k, v in ins.items()]
    out = nc.dram_tensor("out_rows", (tokens, D), F32, kind="ExternalOutput").ap()
    flamingo_block(nc, *aps, out)
    r = run_bass_kernel_spmd(nc, [ins], core_ids=[0])
    return r.results[0]["out_rows"].reshape(shape)
```

```python
from contextlib import ExitStack

import concourse.bass as bass
from concourse import mybir

ALU = mybir.AluOpType
ACT = mybir.ActivationFunctionType
AX = mybir.AxisListType
F32 = mybir.dt.float32
BF16 = mybir.dt.bfloat16
I32 = mybir.dt.int32
U32 = mybir.dt.uint32

P = 128
D = 256
KC = D // P
H = 16
EPS = 1e-5
GB = 4
T8 = 8
T_DVE = 2
E = 8
DE = D + E
RING = 8
ROW = D + 4
C_ID, C_TRI, C_MASK, C_REV, C_BASE, C_TRI8 = 0, P, 2 * P, 2 * P + 8, 2 * P + 16, 2 * P + 24
C_TOK = C_TRI8 + 64
C_NUM = C_TOK + 32
C_BLK = C_NUM + E * 32
C_END = C_BLK + 2


def wait(eng, sem, value):
    if isinstance(value, int) and value <= 0:
        return
    eng.wait_ge(sem, value)


def wait_apart(eng, sem, value, passed):
    if isinstance(value, int) and value <= 0:
        return
    eng.wait_ge(sem, value)
    eng.sem_inc(passed, 1)


class Steps:

    def __init__(self, eng, sem, call, per_call):
        self.eng, self.sem, self.base, self.per, self.at = eng, sem, call * per_call, per_call, 0

    def then(self, ins, passed=None):
        ins.then_inc(self.sem, 1)
        self.at += 1
        assert self.at <= self.per
        if passed is None:
            self.eng.wait_ge(self.sem, self.base + self.at)
        else:
            wait_apart(self.eng, self.sem, self.base + self.at, passed)


def flamingo_block(nc, x, x_t, ctx_t, g_x, g_f, w_kv, w_qg, w_o, wo_t, bg, w1b, w2, b2, consts, out):
    tokens = x.shape[0]
    tiles = tokens // P
    pairs = tiles // 2
    region = P + tokens
    blocks = tiles + E - 1
    last_pair = pairs - 1
    early_tiles = 2 * (last_pair - 2)
    assert RING * P <= early_tiles * P - E * (P - 1)
    x_v = x.rearrange("(p j) d -> p j d", p=P)
    rows = nc.dram_tensor("routed_rows", (E * region, ROW), F32).ap()

    with ExitStack() as stack:
        def sb(name, shape, dt=F32):
            return stack.enter_context(nc.sbuf_tensor("sb_" + name, shape, dt))

        def ps(name, shape):
            return stack.enter_context(nc.psum_tensor("ps_" + name, shape, F32))

        def sem(name):
            return stack.enter_context(nc.semaphore(name))

        cst = sb("cst", [P, C_END])
        wkv = sb("wkv", [P, 2, KC, D])
        wqg = sb("wqg", [P, KC, DE])
        wqg_c = sb("wqg_c", [P, KC, DE])
        wo_sb = sb("wo", [P, KC, D])
        wog = sb("wog", [P, KC, DE])
        mean_w = sb("mean_w", [P, P])
        bg_sb = sb("bg", [P, E])
        w2_sb = sb("w2", [P, E, KC, D])
        b2_sb = sb("b2", [P, E, D])
        gates = sb("gates", [P, 2])
        tg = sb("tg", [P, 2])
        gelu_0 = sb("gelu_0", [P, 2])
        tri = sb("tri", [P, P], BF16)
        ones = sb("ones", [P, P], BF16)
        neg_half = sb("neg_half", [P, 2])
        x_sb = sb("x", [P, tiles, D])
        ct = sb("ct", [P, KC, 2, P])
        st = sb("st", [P, 2, 6])
        mv = sb("mv", [P, 2, 2])
        ve = sb("ve", [P, 2])
        rstd = sb("rstd", [P, 2])
        xt = sb("xt", [P, KC, 2, P])
        q_n = sb("q_n", [P, 2, D])
        xg = sb("xg", [P, pairs, 2, E])
        y_q = sb("y_q", [P, 32, H])
        y_k = sb("y_k", [P, 32, H])
        y_v = sb("y_v", [P, 32, H])
        qt = sb("qt", [P, 32, H])
        kt = sb("kt", [P, 32, H])
        vt = sb("vt", [P, 32, H])
        kb = sb("kb", [P, 32, T8, H])
        vb = sb("vb", [P, 32, T8, H])
        mx = sb("mx", [P, 2, 32])
        pe_x = sb("pe_x", [P, 2, 512])
        sm = sb("sm", [P, 2, 32])
        rs = sb("rs", [P, 2, 32])
        rt = sb("rt", [P, 2, 32])
        at = sb("at", [P, 2, GB, 4, H])
        om = sb("om", [P, 2, H, 32])
        cn = sb("cn", [P, 2, H, H])
        ot = sb("ot", [P, KC, 2, P])
        xs = [sb(f"xs_{i}", [P, 2, ROW]) for i in range(2)]
        st1 = sb("st1", [P, 2, 6])
        ve1 = sb("ve1", [P, 2])
        lg = sb("lg", [P, 2, E])
        lm = sb("lm", [P, 2])
        le = sb("le", [P, 2, E])
        lw = sb("lw", [P, 2])
        oh = sb("oh", [P, 2, E])
        oh_b = sb("oh_b", [P, 2, E], BF16)
        base = sb("base", [P, E])
        rb = sb("rb", [P, 2, E])
        tot = sb("tot", [P, 2, E])
        pos = sb("pos", [P, 2])
        pos_i = sb("pos_i", [P, 2], U32)
        pad_row = sb("pad_row", [P, ROW])
        nbm = sb("nbm", [P, E, 32])
        nb = sb("nb", [P, E])
        cmm = sb("cmm", [P, E, E])
        cum = sb("cum", [P, 2, E])
        org = sb("org", [P, E])
        fin = sb("fin", [P, E])
        cum_e = sb("cum_e", [P, 2, E])
        taken = sb("taken", [P, E])
        start = sb("start", [P, E])
        past = sb("past", [P, E])
        mine = sb("mine", [P, E])
        at_row = sb("at_row", [P, E])
        slack = sb("slack", [P, E])
        lap = sb("lap", [P, 1])
        lap_d = sb("lap_d", [P, 32], BF16)
        skip = sb("skip", [P, 64])
        tab_f = sb("tab_f", [P, 2, 32])
        tab_t = sb("tab_t", [P, 2, 32])
        tab = sb("tab", [P, 2, 64], I32)
        w1_sb = [sb(f"w1_{i}", [P, KC * D + KC]) for i in range(RING)]
        xb = [sb(f"xb_{i}", [P, ROW]) for i in range(RING)]
        xbn = [sb(f"xbn_{i}", [P, D]) for i in range(2)]
        xbt = [sb(f"xbt_{i}", [P, KC, P]) for i in range(2)]
        ht = [sb(f"ht_{i}", [P, KC, P]) for i in range(2)]
        yo = [sb(f"yo_{i}", [P, D]) for i in range(2)]
        yf = [sb(f"yf_{i}", [P, D]) for i in range(2)]
        tok_i = [sb(f"tok_i_{i}", [P, 1], U32) for i in range(2)]

        tr = [ps(f"tr{i}", [P, 512]) for i in range(2)]
        pr = ps("pr", [P, 1024])
        so = ps("so", [P, 1024])
        qg = ps("qg", [P, 1024])
        rank_ps = qg[:, DE:DE + 4 * E]

        cst_in, gate_in, late_in = sem("cst_in"), sem("gate_in"), sem("late_in")
        wk_in, wv_in, wq_in, wo_in = sem("wk_in"), sem("wv_in"), sem("wq_in"), sem("wo_in")
        x_in, xt_in, ct_in = sem("x_in"), sem("xt_in"), sem("ct_in")
        setup_step, consts_ok, zero_ok = sem("setup_step"), sem("consts_ok"), sem("zero_ok")
        tanh_ok, mean_done, wqg_ok = sem("tanh_ok"), sem("mean_done"), sem("wqg_ok")
        wog_done, wog_ok = sem("wog_done"), sem("wog_ok")
        passed_dve, passed_pool = sem("passed_dve"), sem("passed_pool")
        ln_step, ln_var, ln_pow, qn_done = sem("ln_step"), sem("ln_var"), sem("ln_pow"), sem("qn_done")
        q_done, k_done, v_done = sem("q_done"), sem("k_done"), sem("v_done")
        yq_out, yk_out, yv_out = sem("yq_out"), sem("yk_out"), sem("yv_out")
        qt_done, kt_done, vt_done = sem("qt_done"), sem("kt_done"), sem("vt_done")
        qt_out, kt_out, vt_out = sem("qt_out"), sem("kt_out"), sem("vt_out")
        kb_done, vb_done = sem("kb_done"), sem("vb_done")
        score_done = sem("score_done")
        max_done, sub_done, exp_done = sem("max_done"), sem("sub_done"), sem("exp_done")
        at_done, at_out = sem("at_done"), sem("at_out")
        sum_done, inv_done, rt_done = sem("sum_done"), sem("inv_done"), sem("rt_done")
        av_done = sem("av_done")
        om_done = sem("om_done")
        cn_done, ot_done, ot_out, wo_done = sem("cn_done"), sem("ot_done"), sem("ot_out"), sem("wo_done")
        res_step, res_var, res_pow = sem("res_step"), sem("res_var"), sem("res_pow")
        pick_step, oh_done, rank_done = sem("pick_step"), sem("oh_done"), sem("rank_done")
        pos_step, rank_read, pos_done = sem("pos_step"), sem("rank_read"), sem("pos_done")
        routed = sem("routed")
        pad_in = sem("pad_in")
        tab_step, tab_done, turned = sem("tab_step"), sem("tab_done"), sem("turned")
        left_done, taken_step, lap_step = sem("left_done"), sem("taken_step"), sem("lap_step")
        lap_done, lap_spread = sem("lap_done"), sem("lap_spread")
        xb_in = [sem(f"xb_in{i}") for i in range(RING)]
        w1_in = [sem(f"w1_in{i}") for i in range(RING)]
        xbn_done, xbt_done, xbt_out = sem("xbn_done"), sem("xbt_done"), sem("xbt_out")
        h_done, gelu_done = sem("h_done"), sem("gelu_done")
        y_done, yb_done, yf_done = sem("y_done"), sem("yb_done"), sem("yf_done")
        stored = [sem(f"stored{i}") for i in range(2)]

        ident = cst[:, C_ID:C_ID + P]

        block = stack.enter_context(nc.Block())

        def slots(eng, pre, slot):
            pre()
            slot(0, 0)
            slot(1, 1)
            with eng.Fori(1, pairs // 2 - 1) as turn:
                slot(2 * turn, 0)
                slot(2 * turn + 1, 1)
            for k in range(pairs - 2, pairs):
                slot(k, k % 2)

        def has(k, shift):
            return not isinstance(k, int) or 0 <= k + shift < pairs

        def block_slots(eng, slot, skew):
            with eng.Fori(1, blocks // RING) as turn:
                for q in range(RING):
                    slot(RING * turn + q, q, turn)
            for b in range(blocks - blocks % RING, blocks + skew):
                slot(b, b % RING, b // RING)

        def divide(eng, n, s):
            if s == 0:
                eng.wait_ge(rt_done, n + 1)
                wait(eng, ot_done, n)
            ins = eng.tensor_tensor(cn[:, s], om[:, s, :, 0:H],
                                    rt[:, s, 0:H].unsqueeze(1).broadcast_to([P, H, H]), ALU.mult)
            if s == 1:
                ins.then_inc(cn_done, 1)

        def fetch_w1(eng, b, q):
            ex = eng.value_load(tab[0:1, 1, bass.ds(b, 1)], min_val=0, max_val=E - 1)
            wait(eng, gelu_done, b - RING + 1)
            eng.dma_start(w1_sb[q][:], w1b[bass.ds(ex, 1)].rearrange("a p f -> p (a f)")).then_inc(w1_in[q], 16)

        def act_fetches(b, q):
            return q % 2 == 1 and not (isinstance(b, int) and b < RING)

        @block.sync
        def _(sp):
            def load_x(n):
                sp.wait_ge(x_in, 16 * n)
                sp.dma_start(x_sb[:, bass.ds(2 * n, 2), :], x_v[:, bass.ds(2 * n, 2), :]).then_inc(x_in, 16)

            def load(n):
                if has(n, 1):
                    load_x(n + 1)
                sp.wait_ge(v_done, n)
                sp.dma_start(ct[:].rearrange("p a b c -> p (a b c)"),
                             ctx_t[bass.ds(n, 1)].rearrange("a p f -> p (a f)")).then_inc(ct_in, 16)
                sp.wait_ge(q_done, n)
                sp.dma_start(xt[:].rearrange("p a b c -> p (a b c)"),
                             x_t[bass.ds(n, 1)].rearrange("a p f -> p (a f)")).then_inc(xt_in, 16)

            sp.dma_start(ct[:].rearrange("p a b c -> p (a b c)"), ctx_t[0]).then_inc(ct_in, 16)
            sp.dma_start(wkv[:, 0], w_kv[:, 0]).then_inc(wk_in, 16)
            sp.dma_start(wkv[:, 1], w_kv[:, 1]).then_inc(wv_in, 16)
            sp.dma_start(wqg[:], w_qg).then_inc(wq_in, 16)
            sp.dma_start(cst[:], consts).then_inc(cst_in, 16)
            sp.dma_start(x_sb[:, 0:2, :], x_v[:, 0:2, :]).then_inc(x_in, 16)
            sp.dma_start(xt[:].rearrange("p a b c -> p (a b c)"), x_t[0]).then_inc(xt_in, 16)
            sp.dma_start(gates[:, 0:1], g_x.partition_broadcast(P)).then_inc(gate_in, 16)
            sp.dma_start(gates[:, 1:2], g_f.partition_broadcast(P)).then_inc(gate_in, 16)
            sp.dma_start(bg_sb[:], bg.partition_broadcast(P)).then_inc(gate_in, 16)
            sp.dma_start(wo_sb[:], w_o).then_inc(wo_in, 16)
            sp.dma_start(wog[:, :, 0:D], wo_t).then_inc(wo_in, 16)
            load_x(1)
            load(1)
            load(2)
            sp.wait_ge(consts_ok, 1)
            sp.dma_start(rows.rearrange("(e r) w -> r e w", e=E)[0:P],
                         pad_row[:].unsqueeze(1).broadcast_to([P, E, ROW])).then_inc(pad_in, 16)
            sp.dma_start(w2_sb[:], w2).then_inc(late_in, 16)
            sp.dma_start(b2_sb[:].rearrange("p e d -> p (e d)"), b2.partition_broadcast(P)).then_inc(late_in, 16)
            with sp.Fori(3, pairs - 1) as n:
                load(n)
            load(pairs - 1)

            def fetch(b, q, turn):
                row = sp.value_load(tab[0:1, 0, bass.ds(b, 1)], min_val=0, max_val=(E - 1) * region + tokens)
                wait(sp, yf_done, b - RING + 1)
                sp.dma_start(xb[q][:], rows[bass.ds(row, P), :]).then_inc(xb_in[q], 16)
                if not act_fetches(b, q):
                    fetch_w1(sp, b, q)

            sp.wait_ge(tab_done, 1)
            sp.wait_ge(routed, 32 * (last_pair - 2))
            for b in range(RING):
                fetch(b, b, 0)
            sp.wait_ge(tab_done, 2)
            sp.wait_ge(routed, 32 * pairs)
            sp.wait_ge(pad_in, 16)
            block_slots(sp, fetch, 0)
            for i in range(2):
                sp.wait_ge(stored[i], 16 * ((blocks + 1 - i) // 2))

        @block.tensor
        def _(pe):
            def project(src, w, dst, width, done):
                for s in range(2):
                    for kc in range(KC):
                        last = pe.matmul(dst[:, s * 512:s * 512 + width] if width > D else dst[:, s * D:(s + 1) * D],
                                         lhsT=src[:, kc, s, :], rhs=w[:, kc, :],
                                         start=(kc == 0), stop=(kc == KC - 1))
                    if done is wo_done:
                        last.then_inc(done, 1)
                if done is not wo_done:
                    last.then_inc(done, 1)

            def pr_read(n, out_sem):
                if isinstance(n, int) and n < 3:
                    wait(pe, out_sem, n)
                else:
                    pe.wait_ge(res_step, 4 * (n - 3) + 2)

            def project_k(n):
                pe.wait_ge(ct_in, 16 * (n + 1))
                pr_read(n, yk_out)
                project(ct, wkv[:, 0], pr[:, 512:1024], D, k_done)

            def project_v(n):
                pr_read(n, yv_out)
                project(ct, wkv[:, 1], pr[:, 0:512], D, v_done)

            def project_q(n):
                pe.wait_ge(xt_in, 16 * (n + 1))
                wait(pe, qn_done, n)
                wait(pe, yq_out, n)
                wait(pe, rank_read, n - 2)
                project(xt, wqg_c, qg, DE, q_done)

            def transpose_y(y, bank, done):
                for g in range(GB):
                    last = pe.transpose(tr[bank][:, g * P:(g + 1) * P],
                                        y[:, T8 * g:T8 * (g + 1), :].rearrange("p t h -> p (t h)"), ident)
                last.then_inc(done, 1)

            def transpose_k(n):
                pe.wait_ge(yk_out, n + 1)
                wait(pe, qt_out, n)
                transpose_y(y_k, 0, kt_done)

            def transpose_v(n):
                pe.wait_ge(yv_out, n + 1)
                wait(pe, vt_out, n)
                wait(pe, ot_out, n - 1)
                transpose_y(y_v, 1, vt_done)

            def transpose_q(n):
                pe.wait_ge(yq_out, n + 1)
                pe.wait_ge(kt_out, n + 1)
                wait(pe, at_out, 2 * n - 1)
                transpose_y(y_q, 0, qt_done)

            def scores(n):
                pe.wait_ge(qt_out, n + 1)
                pe.wait_ge(kb_done, 2 * n + 2)
                if isinstance(n, int) and n == 0:
                    pe.wait_ge(zero_ok, 1)
                for s in range(2):
                    wait(pe, om_done, 2 * n - 1 + s if not isinstance(n, int) or n > 0 else 0)
                    for g in range(GB):
                        for c in range(4):
                            i = (g * 4 + c) * 2 + s
                            q = s * 512 + g * P
                            last = pe.matmul(so[32 * c:32 * c + H, q:q + P], lhsT=qt[:, i, :],
                                             rhs=kb[:, i, :, :].rearrange("p t j -> p (t j)"),
                                             start=True, stop=True)
                    last.then_inc(score_done, 1)

            def transpose_a(n, s, more):
                pe.wait_ge(exp_done, 2 * n + s + 1)
                if more:
                    pe.wait_ge((kt_out, vt_out)[s], n + 2)
                elif s == 1:
                    pe.wait_ge(ot_out, n)
                for g in range(GB):
                    last = pe.transpose(tr[s][:, g * P:(g + 1) * P],
                                        pe_x[:, s, g * P:(g + 1) * P], ident)
                last.then_inc(at_done, 1)

            def values(n, s):
                pe.wait_ge(vb_done, n + 1)
                pe.wait_ge(at_out, 2 * n + s + 1)
                for g in range(GB):
                    for c in range(4):
                        i = (g * 4 + c) * 2 + s
                        q = s * 512 + g * P
                        last = pe.matmul(so[32 * c:32 * c + H, q:q + P], lhsT=at[:, s, g, c, :],
                                         rhs=vb[:, i, :, :].rearrange("p t h -> p (t h)"),
                                         start=True, stop=True)
                last.then_inc(av_done, 1)

            def transpose_o(n, bank):
                pe.wait_ge(cn_done, n + 1)
                for kc in range(KC):
                    for s in range(2):
                        q = (kc * 2 + s) * P
                        last = pe.transpose(bank[:, q:q + P],
                                            cn[:, s, 8 * kc:8 * kc + 8, :].rearrange("p h i -> p (h i)"), ident)
                last.then_inc(ot_done, 1)

            def project_o(n, more):
                pe.wait_ge(ot_out, n + 1)
                if more:
                    pe.wait_ge(yv_out, n + 3)
                    pe.wait_ge(yk_out, n + 3)
                project(ot, wog, pr, DE, wo_done)

            def ranks(n):
                pe.wait_ge(oh_done, n + 1)
                rhs = oh_b[:].rearrange("p s e -> p (s e)")
                pe.matmul(rank_ps[:, 0:2 * E], lhsT=tri[:], rhs=rhs, start=True, stop=True)
                pe.matmul(rank_ps[:, 2 * E:4 * E], lhsT=ones[:], rhs=rhs, start=True, stop=True).then_inc(rank_done, 1)

            def slot(k, q):
                more = has(k, 1)
                first = isinstance(k, int) and k == 0
                if isinstance(k, int) and k == 1:
                    pe.wait_ge(consts_ok, 1)
                if more and not first:
                    project_k(k + 1)
                if has(k, 0):
                    scores(k)
                if has(k, -1):
                    transpose_o(k - 1, tr[1])
                if has(k, -2):
                    ranks(k - 2)
                if isinstance(k, int) and k == 0:
                    pe.wait_ge(wog_ok, 1)
                if more:
                    project_v(k + 1)
                    transpose_k(k + 1)
                    project_q(k + 1)
                    transpose_v(k + 1)
                if has(k, 0) and not more:
                    transpose_a(k, 0, more)
                if has(k, -1):
                    project_o(k - 1, more)
                if has(k, 0):
                    if more:
                        transpose_a(k, 0, more)
                    transpose_a(k, 1, more)
                if more:
                    transpose_q(k + 1)
                if has(k, 0):
                    values(k, 0)
                    values(k, 1)

            def pre():
                pe.wait_ge(wk_in, 16)
                project_k(0)
                pe.wait_ge(wq_in, 16)
                pe.wait_ge(zero_ok, 1)
                for kc in range(KC):
                    last = pe.matmul(qg[:, 0:DE], lhsT=mean_w[:], rhs=wqg[:, kc, :], start=(kc == 0), stop=(kc == KC - 1))
                last.then_inc(mean_done, 1)
                pe.wait_ge(wv_in, 16)
                project_v(0)
                pe.wait_ge(cst_in, 16)
                transpose_k(0)
                pe.wait_ge(wqg_ok, 1)
                project_q(0)
                transpose_v(0)
                pe.wait_ge(wo_in, 32)
                for hc in range(KC):
                    for kc in range(KC):
                        last = pe.matmul(pr[:, hc * E:(hc + 1) * E], lhsT=wo_sb[:, kc, hc * P:(hc + 1) * P],
                                         rhs=wqg_c[:, kc, D:DE], start=(kc == 0), stop=(kc == KC - 1))
                last.then_inc(wog_done, 1)
                project_k(1)
                transpose_q(0)

            slots(pe, pre, slot)

            def transpose_b(b, i):
                pe.wait_ge(xbn_done, b + 1)
                wait(pe, xbt_out, b - 1)
                for kc in range(KC):
                    last = pe.transpose(tr[i][:, kc * P:(kc + 1) * P], xbn[i][:, kc * P:(kc + 1) * P], ident)
                last.then_inc(xbt_done, 1)

            def layer1(b, q, turn):
                i = q % 2
                pe.wait_ge(xbt_out, b + 1)
                pe.wait_ge(w1_in[q], 16 * (turn + 1))
                wait(pe, gelu_done, b - 1)
                if isinstance(b, int) and b < 2:
                    pe.wait_ge(om_done, 2 * last_pair + b + 1)
                for ic in range(KC):
                    for kc in range(KC):
                        last = pe.matmul(so[:, 512 * i + ic * P:512 * i + (ic + 1) * P],
                                         lhsT=w1_sb[q][:, kc * D + ic * P:kc * D + (ic + 1) * P],
                                         rhs=xbt[i][:, kc, :], start=(kc == 0), stop=(kc == KC - 1))
                last.then_inc(h_done, 1)

            def layer2(b, i):
                ex = pe.value_load(tab[0:1, 1, bass.ds(b, 1)], min_val=0, max_val=E - 1)
                pe.wait_ge(gelu_done, b + 1)
                wait(pe, yb_done, b - 1)
                if isinstance(b, int) and b < 2:
                    pe.wait_ge(res_step, 4 * last_pair + b + 1)
                for ic in range(KC):
                    last = pe.matmul(pr[:, 512 * i:512 * i + D], lhsT=ht[i][:, ic, :],
                                     rhs=w2_sb[:, bass.ds(ex, 1), ic, :].rearrange("p a d -> p (a d)"),
                                     start=(ic == 0), stop=(ic == KC - 1))
                last.then_inc(y_done, 1)

            def expert_slot(b, q, turn):
                i = q % 2
                known = isinstance(b, int)
                if not known or b < blocks:
                    layer1(b, q, turn)
                if not known or b > 0:
                    layer2(b - 1, 1 - i)
                if not known or b + 2 < blocks:
                    transpose_b(b + 2, i)

            pe.wait_ge(late_in, 32)
            pe.wait_ge(tab_done, 1)
            transpose_b(0, 0)
            transpose_b(1, 1)
            layer1(0, 0, 0)
            transpose_o(last_pair, qg[:, 512:1024])
            ranks(last_pair - 1)
            transpose_b(2, 0)
            project_o(last_pair, False)
            for b in range(1, RING):
                if b == 3:
                    layer1(3, 3, 0)
                    ranks(last_pair)
                    layer2(2, 0)
                    transpose_b(5, 1)
                else:
                    expert_slot(b, b, 0)
                if b == RING - 2:
                    pe.wait_ge(lap_done, 1)
                    pe.matmul(qg[:, 0:32], lhsT=ones[:], rhs=lap_d[:], start=True, stop=True).then_inc(lap_spread, 1)
            block_slots(pe, expert_slot, 1)

        @block.scalar
        def _(act):
            def scale_q(n):
                act.wait_ge(q_done, n + 1)
                act.wait_ge(ln_pow, n + 1)
                wait(act, yq_out, n)
                for s in range(2):
                    last = act.activation(q_n[:, s, :], qg[:, 512 * s:512 * s + D], ACT.Copy, scale=rstd[:, s:s + 1])
                last.then_inc(qn_done, 1)

            def copy_qt(n):
                act.wait_ge(qt_done, n + 1)
                wait(act, score_done, 2 * n)
                act.copy(qt[:].rearrange("p a b -> p (a b)"), tr[0][:]).then_inc(qt_out, 1)

            def copy_kt(n):
                act.wait_ge(kt_done, n + 1)
                wait(act, kb_done, 2 * n)
                act.copy(kt[:].rearrange("p a b -> p (a b)"), tr[0][:]).then_inc(kt_out, 1)

            def copy_vt(n):
                act.wait_ge(vt_done, n + 1)
                wait(act, vb_done, n)
                act.copy(vt[:].rearrange("p a b -> p (a b)"), tr[1][:]).then_inc(vt_out, 1)

            def spread(dst, src, first, end):
                for t in range(first, end):
                    last = act.activation(dst[:, :, t, :], src[:], ACT.Copy, scale=cst[:, C_MASK + t:C_MASK + t + 1])
                return last

            def spread_k(n, first, end):
                if first == T_DVE:
                    wait(act, score_done, 2 * n)
                    act.wait_ge(kt_out, n + 1)
                last = spread(kb, kt, first, end)
                if end == T8:
                    last.then_inc(kb_done, 1)

            def spread_v(n, first, end):
                if first == 0:
                    wait(act, av_done, 2 * n)
                    act.wait_ge(vt_out, n + 1)
                last = spread(vb, vt, first, end)
                if end == T8:
                    last.then_inc(vb_done, 1)

            def exps(n, s):
                act.wait_ge(sub_done, 2 * n + s + 1)
                act.activation(pe_x[:, s, :], pe_x[:, s, :], ACT.Exp, scale=float(H) ** -0.5).then_inc(exp_done, 1)

            def copy_at(n, s):
                act.wait_ge(at_done, 2 * n + s + 1)
                wait(act, av_done, 2 * n)
                act.copy(at[:, s].rearrange("p g c i -> p (g c) i"),
                         tr[s][:].rearrange("p (q w) -> p q w", w=32)[:, :, 0:H]).then_inc(at_out, 1)

            def copy_ot(n, bank):
                act.wait_ge(ot_done, n + 1)
                wait(act, wo_done, 2 * n)
                act.copy(ot[:].rearrange("p a b c -> p (a b c)"), bank).then_inc(ot_out, 1)

            def slot(k, q):
                more = has(k, 1)
                if isinstance(k, int) and k == pairs - 1:
                    spread_v(k, 0, 5)
                    exps(k, 0)
                    copy_ot(k - 1, tr[1][:])
                    exps(k, 1)
                    copy_at(k, 0)
                    spread_v(k, 5, T8)
                    copy_at(k, 1)
                    return
                if has(k, 0):
                    spread_v(k, 0, T8)
                    exps(k, 0)
                if has(k, -1):
                    copy_ot(k - 1, tr[1][:])
                if has(k, 0):
                    exps(k, 1)
                if more:
                    copy_kt(k + 1)
                    spread_k(k + 1, T_DVE, 4)
                    scale_q(k + 1)
                    copy_vt(k + 1)
                    spread_k(k + 1, 4, 5)
                if has(k, 0):
                    copy_at(k, 0)
                    copy_at(k, 1)
                if more:
                    spread_k(k + 1, 5, 6)
                    copy_qt(k + 1)
                    spread_k(k + 1, 6, T8)

            def pre():
                copy_kt(0)
                spread_k(0, T_DVE, 5)
                scale_q(0)
                spread_k(0, 5, T8)
                copy_vt(0)
                copy_qt(0)
                act.wait_ge(gate_in, 48)
                act.activation(tg[:], gates[:], ACT.Tanh).then_inc(tanh_ok, 1)

            slots(act, pre, slot)

            def expert_slot(b, q, turn):
                i = q % 2
                known = isinstance(b, int)
                if not known or b < blocks:
                    gelu(b, q)
                if not known or b + 2 < blocks:
                    copy_xbt(b + 2, i)
                ahead = 3
                if (not known or b + ahead < blocks) and act_fetches(b + ahead, (q + ahead) % RING):
                    fetch_w1(act, b + ahead, (q + ahead) % RING)

            def gelu(b, q):
                i = q % 2
                act.wait_ge(h_done, b + 1)
                wait(act, y_done, b - 1)
                for ic in range(KC):
                    last = act.activation(ht[i][:, ic, :], so[:, 512 * i + ic * P:512 * i + (ic + 1) * P], ACT.Gelu,
                                          bias=w1_sb[q][:, KC * D + ic:KC * D + ic + 1])
                last.then_inc(gelu_done, 1)

            def copy_xbt(b, i):
                act.wait_ge(xbt_done, b + 1)
                wait(act, h_done, b - 1)
                act.copy(xbt[i][:].rearrange("p a b -> p (a b)"), tr[i][:, 0:KC * P]).then_inc(xbt_out, 1)

            act.activation(gelu_0[:], tg[:], ACT.Gelu)
            copy_xbt(0, 0)
            copy_xbt(1, 1)
            gelu(0, 0)
            copy_ot(last_pair, qg[:, 512:1024])
            copy_xbt(2, 0)
            for b in range(1, RING):
                if b == RING - 2:
                    act.wait_ge(tab_done, 2)
                expert_slot(b, b, 0)
            block_slots(act, expert_slot, 0)

        @block.vector
        def _(dve):
            def stats_x_1(n):
                dve.wait_ge(x_in, 16 * (n + 1))
                for s in range(2):
                    last = dve.bn_stats(st[:, s, :], x_sb[:, bass.ds(2 * n + s, 1), :].rearrange("p a d -> p (a d)"))
                last.then_inc(ln_step, 1)

            def stats_x_2(n):
                wait_apart(dve, ln_step, 2 * n + 1, passed_dve)
                for s in range(2):
                    last = dve.bn_aggr(mv[:, s, :], st[:, s, :])
                last.then_inc(ln_step, 1)

            def stats_x_3(n):
                dve.wait_ge(ln_step, 2 * n + 2)
                wait(dve, ln_pow, n)
                dve.tensor_scalar(ve[:], mv[:, :, 1], EPS, None, ALU.add).then_inc(ln_var, 1)

            def turn_k(n):
                dve.wait_ge(k_done, n + 1)
                wait(dve, kt_done, n)
                dve.transpose(y_k[:].rearrange("p t h -> p h t"),
                              pr[:, 512:1024].rearrange("p (s h i) -> p h s i", s=2, h=H)).then_inc(yk_out, 1)

            def turn_v(n):
                dve.wait_ge(v_done, n + 1)
                wait(dve, vt_done, n)
                dve.transpose(y_v[:].rearrange("p t j -> p j t"),
                              pr[:, 0:512].rearrange("p (s h j) -> p j s h", s=2, h=H)).then_inc(yv_out, 1)

            def turn_q(n):
                dve.wait_ge(qn_done, n + 1)
                dve.tensor_copy(xg[:, bass.ds(n, 1)].rearrange("p a s e -> p (a s) e"),
                                qg[:].rearrange("p (s c) -> p s c", s=2)[:, :, D:DE])
                wait(dve, qt_done, n)
                dve.transpose(y_q[:].rearrange("p t h -> p h t"),
                              q_n[:].rearrange("p s (h i) -> p h s i", h=H)).then_inc(yq_out, 1)

            def spread_k(n):
                dve.wait_ge(kt_out, n + 1)
                wait(dve, score_done, 2 * n)
                for t in range(T_DVE):
                    last = dve.tensor_scalar(kb[:, :, t, :], kt[:], cst[:, C_MASK + t:C_MASK + t + 1], None, ALU.mult)
                last.then_inc(kb_done, 1)

            def scores_of(s):
                return so[:, 512 * s:512 * (s + 1)].rearrange("p (t j) -> p t j", j=H)

            def largest(n, s):
                dve.wait_ge(score_done, 2 * n + s + 1)
                dve.tensor_reduce(mx[:, s, :], scores_of(s), AX.X, ALU.max).then_inc(max_done, 1)

            def shift(n, s):
                wait(dve, at_done, 2 * n)
                dve.wait_ge(max_done, 2 * n + s + 1)
                dve.tensor_tensor(pe_x[:, s, :].rearrange("p (t j) -> p t j", j=H), scores_of(s),
                                  mx[:, s, :].unsqueeze(2).broadcast_to([P, 32, H]), ALU.subtract).then_inc(sub_done, 1)

            def sums(n, s):
                dve.wait_ge(exp_done, 2 * n + s + 1)
                dve.tensor_reduce(sm[:, s, :], pe_x[:, s, :].rearrange("p (t j) -> p t j", j=H), AX.X, ALU.add).then_inc(sum_done, 1)

            def invert(n):
                dve.wait_ge(sum_done, 2 * n + 2)
                wait(dve, rt_done, n)
                dve.reciprocal(rs[:], sm[:]).then_inc(inv_done, 1)

            def turn_inverse(n):
                dve.wait_ge(inv_done, n + 1)
                wait(dve, cn_done, n)
                dve.transpose(rt[:].rearrange("p s t -> p (s t)"), rs[:].rearrange("p s t -> p (s t)")).then_inc(rt_done, 1)

            def turn_o(n, s):
                wait(dve, cn_done, n)
                dve.wait_ge(av_done, 2 * n + s + 1)
                dve.transpose(om[:, s], so[:, 512 * s:512 * (s + 1)].rearrange("p (t h) -> p h t", h=H)).then_inc(om_done, 1)

            def residual(n, xs):
                step = Steps(dve, res_step, n, 4)
                wait(dve, routed, 32 * n - 32)
                for s in range(2):
                    dve.wait_ge(wo_done, 2 * n + s + 1)
                    dve.scalar_tensor_tensor(xs[:, s, 0:D], pr[:, 512 * s:512 * s + D], tg[:, 0:1],
                                             x_sb[:, bass.ds(2 * n + s, 1), :].rearrange("p a d -> p (a d)"), ALU.mult, ALU.add)
                    step.then(dve.scalar_tensor_tensor(lg[:, s, :], pr[:, 512 * s + D:512 * s + DE], tg[:, 0:1],
                                                       xg[:, bass.ds(n, 1), s, :].rearrange("p a e -> p (a e)"), ALU.mult, ALU.add))
                    last = dve.bn_stats(st1[:, s, :], xs[:, s, 0:D])
                step.then(last, passed_dve)
                for s in range(2):
                    last = dve.bn_aggr(xs[:, s, D:D + 2], st1[:, s, :])
                step.then(last)
                dve.tensor_scalar(ve1[:], xs[:, :, D + 1], EPS, None, ALU.add).then_inc(res_var, 1)
                dve.tensor_copy(xs[:, :, D + 2], cst[:, bass.ds(C_TOK + 2 * n, 2)])

            def wide(ap):
                return ap.unsqueeze(1).broadcast_to([P, 2, E])

            def deep(ap):
                return ap.unsqueeze(2).broadcast_to([P, 2, E])

            def pick_1(n, xs):
                dve.wait_ge(res_pow, n + 1)
                for s in range(2):
                    last = dve.scalar_tensor_tensor(lg[:, s, :], lg[:, s, :], xs[:, s, D + 1:D + 2],
                                                    bg_sb[:], ALU.mult, ALU.add)
                last.then_inc(pick_step, 1)

            def pick_2(n):
                dve.wait_ge(pick_step, 4 * n + 1)
                dve.tensor_reduce(lm[:], lg[:], AX.X, ALU.max).then_inc(pick_step, 1)

            def pick_3(n):
                dve.wait_ge(pick_step, 4 * n + 2)
                for s in range(2):
                    last = dve.scalar_tensor_tensor(le[:, s, :], lg[:, s, :], lm[:, s:s + 1], cst[:, C_REV:C_REV + E],
                                                    ALU.is_equal, ALU.mult)
                last.then_inc(pick_step, 1)

            def pick_4(n):
                dve.wait_ge(pick_step, 4 * n + 3)
                dve.tensor_reduce(lw[:], le[:], AX.X, ALU.max).then_inc(pick_step, 1)

            def pick_5(n):
                dve.wait_ge(pick_step, 4 * n + 4)
                wait(dve, rank_done, n)
                dve.tensor_tensor(oh[:], le[:], deep(lw[:]), ALU.is_equal)
                dve.tensor_tensor(oh_b[:], le[:], deep(lw[:]), ALU.is_equal).then_inc(oh_done, 1)

            def read_ranks(n):
                dve.wait_ge(rank_done, n + 1)
                dve.tensor_copy(tot[:].rearrange("p s e -> p (s e)"), rank_ps[:, 2 * E:4 * E])
                dve.tensor_tensor(rb[:], rank_ps[:, 0:2 * E].rearrange("p (s e) -> p s e", s=2), wide(base[:]),
                                  ALU.add).then_inc(rank_read, 1)

            def place_1(n):
                dve.wait_ge(rank_read, n + 1)
                dve.tensor_tensor(rb[:, 1, :], rb[:, 1, :], tot[:, 0, :], ALU.add)
                dve.tensor_tensor(base[:], base[:], tot[:, 0, :], ALU.add).then_inc(pos_step, 1)

            def place_2(n):
                dve.wait_ge(pos_step, 3 * n + 1)
                dve.tensor_tensor(rb[:], rb[:], oh[:], ALU.mult)
                dve.tensor_tensor(base[:], base[:], tot[:, 1, :], ALU.add).then_inc(pos_step, 1)

            def place_3(n):
                dve.wait_ge(pos_step, 3 * n + 2)
                dve.tensor_reduce(pos[:], rb[:], AX.X, ALU.add).then_inc(pos_step, 1)

            def place_4(n):
                dve.wait_ge(pos_step, 3 * n + 3)
                wait(dve, routed, 32 * n)
                dve.tensor_copy(pos_i[:], pos[:]).then_inc(pos_done, 1)

            b_num, b_rows = cst[:, C_BLK:C_BLK + 1], cst[:, C_BLK + 1:C_BLK + 2]

            def tab_wait(which, step):
                dve.wait_ge(tab_step, 8 * which + step)

            def tab_1(which, pairs_placed):
                dve.wait_ge(pos_step, 3 * pairs_placed - 1)
                dve.tensor_scalar(fin[:], base[:], -float(P), None, ALU.add)
                dve.scalar_tensor_tensor(nbm[:], base[:].unsqueeze(2).broadcast_to([P, E, 32]), (1.0 - P, 0.0)[which],
                                         cst[:, C_NUM:C_NUM + E * 32].rearrange("p (e m) -> p e m", e=E),
                                         ALU.add, ALU.is_gt).then_inc(tab_step, 1)

            def tab_2(which):
                tab_wait(which, 1)
                dve.tensor_reduce(nb[:], nbm[:], AX.X, ALU.add).then_inc(tab_step, 1)

            def tab_2b():
                tab_wait(1, 2)
                dve.tensor_tensor(nb[:], nb[:], taken[:], ALU.subtract).then_inc(left_done, 1)
                dve.wait_ge(left_done, 1)

            def tab_3(which):
                tab_wait(which, 2)
                dve.scalar_tensor_tensor(org[:], nb[:], float(P), start[:] if which else cst[:, C_BASE:C_BASE + E],
                                         ALU.mult, ALU.add)
                dve.tensor_tensor(cmm[:], nb[:].unsqueeze(1).broadcast_to([P, E, E]),
                                  cst[:, C_TRI8:C_TRI8 + 64].rearrange("p (a b) -> p a b", a=E), ALU.mult).then_inc(tab_step, 1)

            def tab_4(which):
                tab_wait(which, 3)
                dve.tensor_reduce(cum[:, 0, :], cmm[:], AX.X, ALU.add).then_inc(tab_step, 1)

            def tab_5(which):
                tab_wait(which, 4)
                dve.tensor_scalar(past[:], cum[:, 0, :], b_num, None, ALU.is_le)
                dve.scalar_tensor_tensor(org[:], cum[:, 0, :], -float(P), org[:], ALU.mult, ALU.add)
                dve.tensor_tensor(cum[:, 1, :], cum[:, 0, :], nb[:], ALU.subtract).then_inc(tab_step, 1)

            def tab_6(which):
                tab_wait(which, 5)
                dve.tensor_tensor(slack[:], org[:], fin[:], ALU.subtract)
                dve.tensor_reduce(tab_f[:, 1, 0:1], past[:], AX.X, ALU.add)
                dve.scalar_tensor_tensor(at_row[:], org[:], b_rows, fin[:], ALU.add, ALU.min)
                dve.scalar_tensor_tensor(mine[:], cum[:, 1, :], b_num, past[:], ALU.is_le, ALU.subtract).then_inc(tab_step, 1)

            def tab_7(which):
                tab_wait(which, 6)
                dve.tensor_scalar(tab_f[:, 1, 0:1], tab_f[:, 1, 0:1], float(E - 1), None, ALU.min)
                dve.tensor_tensor(at_row[:], at_row[:], mine[:], ALU.mult).then_inc(tab_step, 1)

            def tab_8(which):
                tab_wait(which, 7)
                dve.tensor_reduce(tab_f[:, 0, 0:1], at_row[:], AX.X, ALU.add).then_inc(tab_step, 1)

            def tab_9(which):
                tab_wait(which, 8)
                dve.transpose(tab_t[:].rearrange("p a b -> p (a b)"),
                              tab_f[:].rearrange("p a b -> p (a b)")).then_inc(turned, 1)

            def tab_10(which):
                dve.wait_ge(turned, which + 1)
                first, count = ((0, RING), (RING, 32))[which]
                dve.tensor_copy(tab[:, :, first:first + count], tab_t[:, :, 0:count]).then_inc(tab_done, 1)

            def taken_1():
                tab_wait(0, 5)
                dve.tensor_scalar(cum_e[:], cum[:], float(RING), None, ALU.min).then_inc(taken_step, 1)

            def taken_2():
                dve.wait_ge(taken_step, 1)
                dve.tensor_tensor(taken[:], cum_e[:, 0, :], cum_e[:, 1, :], ALU.subtract).then_inc(taken_step, 1)

            def taken_3():
                dve.wait_ge(taken_step, 2)
                dve.scalar_tensor_tensor(start[:], taken[:], float(P), cst[:, C_BASE:C_BASE + E],
                                         ALU.mult, ALU.add).then_inc(taken_step, 1)

            def lap_1():
                dve.wait_ge(tab_done, 2)
                dve.scalar_tensor_tensor(past[:], slack[:], b_rows, mine[:], ALU.add, ALU.mult).then_inc(lap_step, 1)

            def lap_2():
                dve.wait_ge(lap_step, 1)
                dve.tensor_reduce(lap[:], past[:], AX.X, ALU.add).then_inc(lap_step, 1)

            def lap_3():
                dve.wait_ge(lap_step, 2)
                dve.tensor_scalar(lap_d[:], cst[:, C_ID:C_ID + 32], lap[:], None, ALU.mult).then_inc(lap_done, 1)

            def lap_4():
                dve.wait_ge(lap_spread, 1)
                dve.tensor_scalar(skip[:, RING:RING + 32], qg[:, 0:32], b_num, 2.0 * tokens, ALU.is_gt, ALU.mult).then_inc(lap_step, 1)

            def norm_b(b, q, turn):
                i = q % 2
                dve.wait_ge(xb_in[q], 16 * (turn + 1))
                wait(dve, xbt_done, b - 1)
                dve.tensor_scalar(xbn[i][:], xb[q][:, 0:D], xb[q][:, D:D + 1], xb[q][:, D + 1:D + 2],
                                  ALU.subtract, ALU.mult).then_inc(xbn_done, 1)

            def finish(b, q, nth):
                i = q % 2
                ex = dve.value_load(tab[0:1, 1, bass.ds(b, 1)], min_val=0, max_val=E - 1)
                dve.wait_ge(y_done, b + 1)
                wait(dve, stored[i], 16 * nth)
                dve.tensor_tensor(yo[i][:], pr[:, 512 * i:512 * i + D],
                                  b2_sb[:, bass.ds(ex, 1), :].rearrange("p a d -> p (a d)"), ALU.add).then_inc(yb_done, 1)
                dve.tensor_tensor(tok_i[i][:], xb[q][:, D + 2:D + 3], skip[:, bass.ds(b, 1)], ALU.add)
                dve.wait_ge(yb_done, b + 1)
                dve.scalar_tensor_tensor(yf[i][:], yo[i][:], tg[:, 1:2], xb[q][:, 0:D], ALU.mult, ALU.add).then_inc(yf_done, 1)

            def slot(k, q):
                tab_now = isinstance(k, int) and k == last_pair - 1
                if has(k, 1):
                    stats_x_1(k + 1)
                if has(k, -2):
                    pick_4(k - 2)
                if has(k, 0):
                    largest(k, 0)
                if has(k, -2):
                    pick_5(k - 2)
                if has(k, 1):
                    stats_x_2(k + 1)
                if has(k, 0):
                    shift(k, 0)
                    largest(k, 1)
                if has(k, 1):
                    stats_x_3(k + 1)
                    turn_k(k + 1)
                if has(k, 0):
                    shift(k, 1)
                if has(k, -2):
                    read_ranks(k - 2)
                    place_1(k - 2)
                    place_2(k - 2)
                if has(k, 0):
                    sums(k, 0)
                if tab_now:
                    tab_1(0, k - 1)
                if has(k, -2):
                    place_3(k - 2)
                if has(k, 1):
                    turn_v(k + 1)
                if tab_now:
                    tab_2(0)
                if has(k, -2):
                    place_4(k - 2)
                if has(k, 0):
                    sums(k, 1)
                if tab_now:
                    tab_3(0)
                if has(k, 0):
                    invert(k)
                if tab_now:
                    tab_4(0)
                if has(k, 1):
                    turn_q(k + 1)
                if tab_now:
                    tab_5(0)
                if has(k, 0):
                    turn_inverse(k)
                if tab_now:
                    tab_6(0)
                if has(k, 1):
                    spread_k(k + 1)
                if tab_now:
                    tab_7(0)
                if has(k, -1):
                    residual(k - 1, xs[1 - q])
                if tab_now:
                    tab_8(0)
                if isinstance(k, int) and k == last_pair:
                    norm_b(0, 0, 0)
                    norm_b(1, 1, 0)
                if has(k, 0):
                    turn_o(k, 0)
                if tab_now:
                    tab_9(0)
                if has(k, -1):
                    pick_1(k - 1, xs[1 - q])
                if has(k, 0):
                    turn_o(k, 1)
                if tab_now:
                    tab_10(0)
                if isinstance(k, int) and k == last_pair:
                    dve.wait_ge(om_done, 2 * pairs)
                    divide(dve, k, 0)
                    divide(dve, k, 1)
                if has(k, -1):
                    pick_2(k - 1)
                if tab_now:
                    taken_1()
                if has(k, -1):
                    pick_3(k - 1)
                if tab_now:
                    taken_2()
                    taken_3()

            def pre():
                step = Steps(dve, setup_step, 0, 3)
                dve.memset(neg_half[:], -0.5)
                dve.memset(ones[:], 1.0)
                dve.memset(mean_w[:], 1.0 / D)
                for i in range(2):
                    dve.memset(xs[i][:], 0.0)
                dve.memset(tab_f[:], 0.0)
                dve.memset(skip[:], 0.0)
                dve.memset(pad_row[:], 0.0)
                step.then(dve.memset(so[:], 0.0))
                dve.memset(pad_row[:, D + 2:D + 3], 2.0 * tokens)
                dve.sem_inc(zero_ok, 1)
                turn_k(0)
                dve.wait_ge(wq_in, 16)
                dve.wait_ge(mean_done, 1)
                dve.tensor_tensor(wqg_c[:], wqg[:], qg[:, 0:DE].unsqueeze(1).broadcast_to([P, KC, DE]),
                                  ALU.subtract).then_inc(wqg_ok, 1)
                stats_x_1(0)
                stats_x_2(0)
                stats_x_3(0)
                turn_v(0)
                dve.wait_ge(cst_in, 16)
                spread_k(0)
                turn_q(0)
                dve.tensor_copy(tri[:], cst[:, C_TRI:C_TRI + P])
                step.then(dve.tensor_copy(base[:], cst[:, C_BASE:C_BASE + E]))
                dve.sem_inc(consts_ok, 1)
                dve.wait_ge(wo_in, 32)
                dve.wait_ge(wog_done, 1)
                dve.tensor_copy(wog[:, :, D:DE], pr[:, 0:KC * E].rearrange("p (c e) -> p c e", c=KC)).then_inc(wog_ok, 1)
                dve.wait_ge(gate_in, 48)
                dve.wait_ge(tanh_ok, 1)

            slots(dve, pre, slot)

            def expert_slot(b, q, turn):
                known = isinstance(b, int)
                if not known or b + 3 < blocks:
                    norm_b(b + 3, (q + 3) % RING, turn + (q + 3) // RING)
                if not known or b > 0:
                    finish(b - 1, (q - 1) % RING, RING // 2 * turn + (q - 1) // 2)

            dve.wait_ge(late_in, 32)
            n = last_pair - 1
            pick_4(n)
            norm_b(2, 2, 0)
            pick_5(n)
            norm_b(3, 3, 0)
            read_ranks(n)
            place_1(n)
            place_2(n)
            place_3(n)
            place_4(n)
            n = last_pair
            residual(n, xs[n % 2])
            expert_slot(1, 1, 0)
            pick_1(n, xs[n % 2])
            pick_2(n)
            pick_3(n)
            pick_4(n)
            pick_5(n)
            expert_slot(2, 2, 0)
            read_ranks(n)
            place_1(n)
            place_2(n)
            tab_1(1, pairs)
            place_3(n)
            tab_2(1)
            place_4(n)
            tab_2b()
            tab_3(1)
            norm_b(6, 6, 0)
            tab_4(1)
            finish(2, 2, 1)
            tab_5(1)
            tab_6(1)
            tab_7(1)
            tab_8(1)
            tab_9(1)
            tab_10(1)
            expert_slot(4, 4, 0)
            lap_1()
            lap_2()
            lap_3()
            for b in range(5, RING):
                finish(b - 1, b - 1, (b - 1) // 2)
                if b == RING - 1:
                    lap_4()
                norm_b(b + 3, (b + 3) % RING, 1)
            dve.wait_ge(lap_step, 3)
            block_slots(dve, expert_slot, 1)

        @block.gpsimd
        def _(pool):
            def pow_x(n):
                pool.wait_ge(ln_var, n + 1)
                wait(pool, qn_done, n)
                pool.tensor_tensor(rstd[:], ve[:], neg_half[:], ALU.pow).then_inc(ln_pow, 1)

            def pow_x1(n, xs):
                pool.wait_ge(res_var, n + 1)
                pool.tensor_tensor(xs[:, :, D + 1], ve1[:], neg_half[:], ALU.pow).then_inc(res_pow, 1)

            def route(n, xs):
                pool.wait_ge(pos_done, n + 1)
                wait_apart(pool, res_pow, n + 1, passed_pool)
                for s in range(2):
                    pool.indirect_dma_start(rows, bass.IndirectOffsetOnAxis(ap=pos_i[:, s:s + 1], axis=0),
                                            xs[:, s, :], None).then_inc(routed, 16)

            def slot(k, q):
                if has(k, -1) and has(k, 0):
                    pool.wait_ge(om_done, 2 * k)
                    divide(pool, k - 1, 0)
                    divide(pool, k - 1, 1)
                if has(k, 1):
                    pow_x(k + 1)
                if has(k, -2):
                    route(k - 2, xs[q])
                if has(k, -1):
                    pow_x1(k - 1, xs[1 - q])

            def pre():
                pool.wait_ge(zero_ok, 1)
                pow_x(0)

            slots(pool, pre, slot)

            def store(b, q, turn):
                i = q % 2
                wait_apart(pool, yf_done, b + 1, passed_pool)
                pool.indirect_dma_start(out, bass.IndirectOffsetOnAxis(ap=tok_i[i][:, 0:1], axis=0),
                                        yf[i][:], None, bounds_check=tokens - 1, oob_is_err=False).then_inc(stored[i], 16)

            route(last_pair - 1, xs[(last_pair - 1) % 2])
            pow_x1(last_pair, xs[last_pair % 2])
            for b in range(RING):
                store(b, b, 0)
                if b == 1:
                    route(last_pair, xs[last_pair % 2])
            block_slots(pool, store, 0)


def kernel(x, ctx_1024, g_xattn, g_ffn, L0_xattn_Wq, L0_xattn_Wk, L0_xattn_Wv, L0_xattn_Wo, L0_ffn_Wg,
           L0_ffn_bg, L0_ffn_W1, L0_ffn_b1, L0_ffn_W2, L0_ffn_b2):
    import concourse.bacc as bacc
    import numpy as np
    from concourse.bass_utils import run_bass_kernel_spmd

    a = {k: np.asarray(v) for k, v in locals().items() if k in (
        "x", "ctx_1024", "g_xattn", "g_ffn", "L0_xattn_Wq", "L0_xattn_Wk", "L0_xattn_Wv", "L0_xattn_Wo",
        "L0_ffn_Wg", "L0_ffn_bg", "L0_ffn_W1", "L0_ffn_b1", "L0_ffn_W2", "L0_ffn_b2")}
    shape = a["x"].shape
    tokens = shape[0] * shape[1]
    tiles = tokens // P
    pairs = tiles // 2
    region = P + tokens
    def chunked(w):
        return np.moveaxis(w.reshape(w.shape[:-2] + (KC, P, w.shape[-1])), -3, -2)

    ctx_t = a["ctx_1024"].reshape(P, pairs, 2, KC, P).transpose(1, 4, 3, 2, 0).reshape(pairs, P, KC * 2 * P)
    x_t = a["x"].reshape(P, pairs, 2, KC, P).transpose(1, 4, 3, 2, 0).reshape(pairs, P, KC * 2 * P)
    w_kv = np.stack([chunked(a[f"L0_xattn_W{n}"].T) for n in "kv"], axis=1)
    w_qg = chunked(np.concatenate([a["L0_xattn_Wq"].T, a["L0_ffn_Wg"]], axis=1))
    w1 = chunked(a["L0_ffn_W1"]).reshape(E, P, KC * D)
    b1 = a["L0_ffn_b1"].reshape(E, KC, P).transpose(0, 2, 1)
    w1b = np.concatenate([w1, b1], axis=2)
    w2 = chunked(a["L0_ffn_W2"]).transpose(1, 0, 2, 3)

    p = np.arange(P)
    consts = np.zeros((P, C_END), np.float32)
    consts[:, C_ID:C_ID + P] = np.eye(P)
    consts[:, C_TRI:C_TRI + P] = p[:, None] < p[None, :]
    consts[:, C_MASK:C_MASK + T8] = (p[:, None] // H) == np.arange(T8)[None, :]
    consts[:, C_REV:C_REV + E] = E - np.arange(E)
    consts[:, C_BASE:C_BASE + E] = region * np.arange(E) + P
    consts[:, C_TRI8:C_TRI8 + E * E] = (np.arange(E)[None, :] <= np.arange(E)[:, None]).reshape(-1)
    consts[:, C_TOK:C_TOK + tiles] = tiles * p[:, None] + np.arange(tiles)[None, :]
    consts[:, C_NUM:C_NUM + E * 32] = (region * np.arange(E)[:, None] + P + P * np.arange(32)[None, :]).reshape(-1)
    consts[:, C_BLK:C_BLK + 2] = np.stack([p, P * p], axis=1)

    ins = {
        "x_in": a["x"].reshape(tokens, D), "xt_in_": x_t, "ctx_in": ctx_t, "gx_in": a["g_xattn"], "gf_in": a["g_ffn"],
        "wkv_in": w_kv, "wqg_in": w_qg, "wo_in_": chunked(a["L0_xattn_Wo"]),
        "wot_in": chunked(a["L0_xattn_Wo"].T), "bg_in": a["L0_ffn_bg"], "w1_in_": w1b,
        "w2_in": w2, "b2_in": a["L0_ffn_b2"].reshape(-1), "consts_in": consts,
    }
    ins = {k: np.ascontiguousarray(v) for k, v in ins.items()}
    nc = bacc.Bacc("TRN2", target_bir_lowering=False, num_devices=1)
    aps = [nc.dram_tensor(k, v.shape, mybir.dt.from_np(v.dtype), kind="ExternalInput").ap() for k, v in ins.items()]
    out = nc.dram_tensor("out_rows", (tokens, D), F32, kind="ExternalOutput").ap()
    flamingo_block(nc, *aps, out)
    r = run_bass_kernel_spmd(nc, [ins], core_ids=[0])
    return r.results[0]["out_rows"].reshape(shape)
```
